# Optimizing a Trainium2 kernel written in Bass

```python
import numpy as np
import jax
import jax.numpy as jnp

def _softmax(x, axis=-1):
    return jax.nn.softmax(x, axis=axis)

def _gelu(x):
    return jax.nn.gelu(x, approximate=True)

def _silu(x):
    return jax.nn.silu(x)

def _sigmoid(x):
    return jax.nn.sigmoid(x)

def _layernorm(x, axis=-1, eps=1e-05):
    m = jnp.mean(x, axis=axis, keepdims=True)
    v = jnp.var(x, axis=axis, keepdims=True)
    return (x - m) / jnp.sqrt(v + eps)

def _scatter_add(tgt, idx, src, axis=0):
    return tgt.at[idx].add(src)

def _segment_sum(src, seg, n):
    return jax.ops.segment_sum(src, seg, n)
kernel_name = 'mk_gnn_resnorm_d1_gnn_r64_b44a84'

def setup_inputs(seed: int=0):
    np.random.seed(seed)
    _w = jnp.asarray

    def _rec_inputs():
        import jax
        import jax.numpy as jnp
        _gk = jax.random.key(seed)
        x = -0.000202 + 1 * jax.random.normal(jax.random.fold_in(_gk, 1), (100000, 128), jnp.float32)
        src = jax.random.randint(jax.random.fold_in(_gk, 2), (25000,), 0, 100000, jnp.int32)
        dst = jax.random.randint(jax.random.fold_in(_gk, 3), (25000,), 0, 100000, jnp.int32)
        _o = jnp.argsort(dst, stable=True)
        src = src[_o]
        dst = dst[_o]
        return (x, src, dst)
    x, src, dst = _rec_inputs()

    def _L0_gnn_setup():
        import jax, jax.numpy as jnp
        import numpy as np
        N_NODES = 50000
        N_EDGES = 12500
        HID = 128
        key = jax.random.key(seed)
        ks = jax.random.split(key, 10)
        d = HID
        s1 = 1.0 / np.sqrt(2 * d)
        s2 = 1.0 / np.sqrt(d)
        return {'node_features': jax.random.normal(ks[0], (N_NODES, d), dtype=jnp.float32), 'edge_indices': jax.random.randint(ks[1], (N_EDGES, 2), 0, N_NODES, dtype=jnp.int64), 'msg_w1': jax.random.uniform(ks[2], (2 * d, d), jnp.float32, -s1, s1), 'msg_b1': jax.random.uniform(ks[3], (d,), jnp.float32, -s1, s1), 'msg_w2': jax.random.uniform(ks[4], (d, d), jnp.float32, -s2, s2), 'msg_b2': jax.random.uniform(ks[5], (d,), jnp.float32, -s2, s2), 'upd_w1': jax.random.uniform(ks[6], (2 * d, d), jnp.float32, -s1, s1), 'upd_b1': jax.random.uniform(ks[7], (d,), jnp.float32, -s1, s1), 'upd_w2': jax.random.uniform(ks[8], (d, d), jnp.float32, -s2, s2), 'upd_b2': jax.random.uniform(ks[9], (d,), jnp.float32, -s2, s2)}
    _L0_gnn_all = _L0_gnn_setup()
    _L0_gnn_in = {k: v for k, v in _L0_gnn_all.items() if k in ('msg_w1', 'msg_b1', 'msg_w2', 'msg_b2', 'upd_w1', 'upd_b1', 'upd_w2', 'upd_b2')}
    del _L0_gnn_all
    return {'x': x, 'src': src, 'dst': dst, 'L0_gnn_msg_w1': _L0_gnn_in['msg_w1'], 'L0_gnn_msg_b1': _L0_gnn_in['msg_b1'], 'L0_gnn_msg_w2': _L0_gnn_in['msg_w2'], 'L0_gnn_msg_b2': _L0_gnn_in['msg_b2'], 'L0_gnn_upd_w1': _L0_gnn_in['upd_w1'], 'L0_gnn_upd_b1': _L0_gnn_in['upd_b1'], 'L0_gnn_upd_w2': _L0_gnn_in['upd_w2'], 'L0_gnn_upd_b2': _L0_gnn_in['upd_b2']}

def reference(x, src, dst, L0_gnn_msg_w1, L0_gnn_msg_b1, L0_gnn_msg_w2, L0_gnn_msg_b2, L0_gnn_upd_w1, L0_gnn_upd_b1, L0_gnn_upd_w2, L0_gnn_upd_b2):
    import jax
    import jax.numpy as jnp

    def _L0_gnn_ref(node_features, edge_indices, msg_w1, msg_b1, msg_w2, msg_b2, upd_w1, upd_b1, upd_w2, upd_b2):
        import jax, jax.numpy as jnp
        import numpy as np
        N_NODES = 50000
        N_EDGES = 12500
        HID = 128
        src = edge_indices[:, 0]
        dst = edge_indices[:, 1]
        edge_input = jnp.concatenate([node_features[src], node_features[dst]], axis=-1)
        h = jax.nn.relu(edge_input @ msg_w1 + msg_b1)
        message = h @ msg_w2 + msg_b2
        messages = jax.ops.segment_sum(message, dst, num_segments=node_features.shape[0])
        update_input = jnp.concatenate([node_features, messages], axis=-1)
        u = jax.nn.relu(update_input @ upd_w1 + upd_b1)
        return u @ upd_w2 + upd_b2
    edge_index_t = jnp.stack([src, dst], axis=1)
    x = _layernorm(x + _L0_gnn_ref(x, edge_index_t, L0_gnn_msg_w1, L0_gnn_msg_b1, L0_gnn_msg_w2, L0_gnn_msg_b2, L0_gnn_upd_w1, L0_gnn_upd_b1, L0_gnn_upd_w2, L0_gnn_upd_b2), axis=-1)
    return x

_drawn_inputs = setup_inputs


def setup_inputs(seed=0):
    import zlib

    import numpy as np

    out = dict(_drawn_inputs(seed))
    spreads = {}
    factors = {'L0_gnn_msg_w1': 3.481,
     'L0_gnn_msg_b1': 8.0,
     'L0_gnn_msg_w2': 2.77,
     'L0_gnn_msg_b2': 8.0,
     'L0_gnn_upd_b1': 3.846}
    for name, (base, spread) in spreads.items():
        noise = np.random.default_rng([zlib.crc32(name.encode()), seed]).standard_normal(out[name].shape)
        drawn = base * np.exp(spread * noise) if base else spread * noise
        out[name] = jnp.asarray(drawn.astype(out[name].dtype))
    for name, factor in factors.items():
        out[name] = (out[name] * factor).astype(out[name].dtype)
    return out
```

```python
from contextlib import ExitStack

import numpy as np
import concourse.bass as bass
from concourse import mybir

ALU = mybir.AluOpType
ACT = mybir.ActivationFunctionType
F32 = mybir.dt.float32
BF16 = mybir.dt.bfloat16
I32 = mybir.dt.int32

P = 128
QUAD = 4
W = QUAD * P
ROWS = 16
NODES = P * ROWS
EDGES = W
NQ = ROWS // QUAD
RING = 4
PEEL = 5
EPS = 1e-5

TURNS = {0: 0, 1: 1, "src": 2, "dst": 3, 2: 4, 3: 5}
N_TURNS = len(TURNS)
OUTS = {0: 0, 1: 1, 2: 2, 3: 3, "edge": 4}
N_OUTS = len(OUTS)
BLOCKS = ROWS + QUAD
ACT_NORM = 12


def gnn_resnorm(nc, x, src, dst, msg_w1, msg_b1, msg_w2, msg_b2, upd_w1, upd_b1, upd_w2, upd_b2, out):
    N, D = x.shape
    E = src.shape[0]
    GROUPS = -(-N // NODES)
    SHORT = GROUPS * NODES - N
    E_PAD = GROUPS * EDGES
    assert D == P and E_PAD >= E and (GROUPS - PEEL) % RING == 0 and SHORT % ROWS == 0
    LOOPS = (GROUPS - PEEL) // RING
    FAR = 1 << 20
    CHECKED = GROUPS - 2
    SPLIT = 10
    assert E % SPLIT == 0 and N < FAR

    src_pad = nc.dram_tensor("src_pad", [E_PAD], I32).ap()
    dst_pad = nc.dram_tensor("dst_pad", [E_PAD + 2], I32).ap()
    kept_rows = nc.dram_tensor("kept_rows", [GROUPS * P, QUAD * P], F32).ap()
    kept_index = nc.dram_tensor("kept_index", [GROUPS * P, QUAD], I32).ap()

    with ExitStack() as ctx:
        def sb(name, shape, dt=F32):
            return ctx.enter_context(nc.sbuf_tensor(name, shape, dt))

        def sem(name):
            return ctx.enter_context(nc.semaphore(name))

        def sems(name):
            return [sem(f"{name}{q}") for q in range(RING)]

        turned_ps = ctx.enter_context(nc.psum_tensor("turned_ps", [P, 2, W], F32))
        pre_ps = ctx.enter_context(nc.psum_tensor("pre_ps", [P, 2, W], F32))
        out_ps = ctx.enter_context(nc.psum_tensor("out_ps", [P, 2, W], F32))
        edge_ps = ctx.enter_context(nc.psum_tensor("edge_ps", [P, 2, W], F32))

        w_src, w_dst, w_x, w_m, w_msg2, w_msg2T, w_fold, w_out, ident = (
            sb(n, [P, P]) for n in
            ("w_src", "w_dst", "w_x", "w_m", "w_msg2", "w_msg2T", "w_fold", "w_out", "ident"))
        b_h, b_msg2, b_fold, b_u, eps = (sb(n, [P, 1]) for n in ("b_h", "b_msg2", "b_fold", "b_u", "eps"))
        b_row = sb("b_row", [1, 3, P])
        b_split = sb("b_split", [1, 3, QUAD, P], BF16)
        b_parts = sb("b_parts", [3, W], BF16)
        ones = sb("ones", [3, P], BF16)
        zeros_i = sb("zeros_i", [1, P], I32)
        ends_i = sb("ends_i", [1, 2 * P], I32)

        node_x = sb("node_x", [P, RING, ROWS, P])
        node_z = sb("node_z", [P, RING, ROWS, P])
        src_i = sb("src_i", [P, RING, QUAD], I32)
        dst_i = sb("dst_i", [P, RING, QUAD + 1], I32)
        dst_row = sb("dst_row", [P, RING, W + 1], I32)
        src_x = sb("src_x", [P, RING, QUAD, P])
        dst_x = sb("dst_x", [P, RING, QUAD, P])
        edge_z = sb("edge_z", [P, RING, QUAD, P])
        out_i = sb("out_i", [P, RING, QUAD], I32)
        same_i = sb("same_i", [P, QUAD], I32)

        node_xT = sb("node_xT", [P, 2, W])
        node_u = sb("node_u", [P, 2, W])
        src_xT = sb("src_xT", [P, W])
        dst_xT = sb("dst_xT", [P, W])
        edge_h = sb("edge_h", [P, W])
        edge_m = sb("edge_m", [P, W])
        same = sb("same", [P, W])
        summed = sb("summed", [P, 2, W])
        edge_pre = sb("edge_pre", [P, W])
        edge_u = sb("edge_u", [P, W])

        stats = sb("stats", [P, 2, BLOCKS, 6])
        mean2, diff, spread, diff2, var, std, scale, shift = (
            sb(n, [P, BLOCKS]) for n in
            ("mean2", "diff", "spread", "diff2", "var", "std", "scale", "shift"))

        back_rows = sb("back_rows", [P, QUAD, P])
        back_i = sb("back_i", [P, QUAD], I32)

        weights_in = sem("weights_in")
        waits_passed = sem("waits_passed")
        ident_made, pads_made, edges_ready = (sem(n) for n in ("ident_made", "pads_made", "edges_ready"))
        consts_made, split_made, rest_made, parts_in = (
            sem(n) for n in ("consts_made", "split_made", "rest_made", "parts_in"))
        set_pe, set_act = sem("set_pe"), sem("set_act")
        x_in, z_stored = sems("x_in"), sems("z_stored")
        src_i_in, dst_i_in, dst_row_in = sems("src_i_in"), sems("dst_i_in"), sems("dst_row_in")
        src_gathered, dst_gathered, scattered = sems("src_gathered"), sems("dst_gathered"), sems("scattered")
        turned, turn_copied = sem("turned"), sem("turn_copied")
        pre_done, u_done = sem("pre_done"), sem("u_done")
        out_done, z_done, stats_done = sem("out_done"), sem("z_done"), sem("stats_done")
        h_pre, h_done, m_pre, m_done = (sem(n) for n in ("h_pre", "h_done", "m_pre", "m_done"))
        same_done, sum_done, edge_pre_ps, edge_pre_done, edge_u_done = (
            sem(n) for n in ("same_done", "sum_done", "edge_pre_ps", "edge_pre_done", "edge_u_done"))
        same_i_done, out_i_done = sem("same_i_done"), sem("out_i_done")
        halves_done, square_done, var_done, std_done, scale_done, shift_done = (
            sem(n) for n in ("halves_done", "square_done", "var_done", "std_done", "scale_done", "shift_done"))
        act_normed, dve_normed = sem("act_normed"), sem("dve_normed")
        back_in, back_out = sem("back_in"), sem("back_out")

        def first_node(g):
            return 0 if isinstance(g, int) and g == 0 else NODES * g - SHORT

        def use(i, r):
            return i + r // RING + 1

        def wait(eng, s, value):
            if not isinstance(value, int) or value > 0:
                eng.wait_ge(s, value)

        def wait_alone(eng, s, value):
            wait(eng, s, value)
            if not isinstance(value, int):
                eng.sem_inc(waits_passed, 1)

        def all_groups(eng, group):
            for r in range(PEEL):
                group(0, r)
            with eng.Fori(0, LOOPS) as i:
                for r in range(PEEL, PEEL + RING):
                    group(i, r)

        def block_of(q, b):
            return node_z[:, q, b, :] if b < ROWS else edge_z[:, q, b - ROWS, :]

        def stores_of(q):
            return 16 * sum(1 for g in range(GROUPS) if g % RING == q) + 16 * (q == 0)

        block = ctx.enter_context(nc.Block())

        @block.sync
        def _(sp):
            def load_x(i, r):
                g, q = RING * i + r, r % RING
                wait(sp, z_done, N_OUTS * (g - RING) + OUTS[3] + 1)
                rows = x[bass.ds(first_node(g), NODES), :].rearrange("(p j) f -> p j f", j=ROWS)
                sp.dma_start(node_x[:, q], rows).then_inc(x_in[q], 16)

            def load_edges(i, r):
                g, q = RING * i + r, r % RING
                if not isinstance(g, int) or g >= RING:
                    wait_alone(sp, src_gathered[q], 16 * QUAD * (use(i, r) - 1))
                    wait_alone(sp, dst_gathered[q], 16 * QUAD * (use(i, r) - 1))
                    sp.wait_ge(out_i_done, g - RING + 1)
                    sp.wait_ge(same_done, g - RING + 1)
                s = src_pad[bass.ds(EDGES * g, EDGES)].rearrange("(p j) -> p j", j=QUAD)
                sp.dma_start(src_i[:, q, :], s).then_inc(src_i_in[q], 16)
                d = dst_pad[bass.ds(EDGES * g + 1, EDGES)].rearrange("(p j) -> p j", j=QUAD)
                sp.dma_start(dst_i[:, q, 0:QUAD], d).then_inc(dst_i_in[q], 16)
                n = dst_pad[bass.ds(EDGES * g + 2, EDGES)].rearrange("(p j) -> p j", j=QUAD)
                with nc.allow_non_contiguous_dma(reason="one index in a partition"):
                    sp.dma_start(dst_i[:, q, QUAD:], n[:, QUAD - 1:]).then_inc(dst_i_in[q], 16)
                row = dst_pad[bass.ds(EDGES * g, W + 1)].rearrange("(a w) -> a w", a=1).partition_broadcast(P)
                sp.dma_start(dst_row[:, q, :], row).then_inc(dst_row_in[q], 16)

            def store(i, r):
                g, q = RING * i + r, r % RING
                sp.wait_ge(act_normed, g + 1)
                sp.wait_ge(dve_normed, g + 1)
                if isinstance(g, int) and g == 0:
                    full = (NODES - SHORT) // ROWS
                    for a, b in ((0, full // 8 * 8), (full // 8 * 8, full)):
                        rows = out[a * ROWS:b * ROWS, :].rearrange("(p j) f -> p j f", j=ROWS)
                        sp.dma_start(rows, node_z[a:b, q]).then_inc(z_stored[q], 16)
                    return
                rows = out[bass.ds(first_node(g), NODES), :].rearrange("(p j) f -> p j f", j=ROWS)
                sp.dma_start(rows, node_z[:, q]).then_inc(z_stored[q], 16)

            def lists(name):
                return name.rearrange("(a b) -> a b", a=SPLIT)
            load_x(0, 0)
            sp.dma_start(lists(src_pad[0:E]), lists(src)).then_inc(edges_ready, 16)
            sp.dma_start(lists(dst_pad[1:E + 1]), lists(dst)).then_inc(edges_ready, 16)
            sp.wait_ge(pads_made, 3)
            n_pad = E_PAD - E
            sp.dma_start(src_pad[E:E_PAD].rearrange("(a b) -> a b", a=1), zeros_i[:, 0:n_pad]).then_inc(edges_ready, 16)
            sp.dma_start(dst_pad[0:1].rearrange("(a b) -> a b", a=1), ends_i[:, 0:1]).then_inc(edges_ready, 16)
            sp.dma_start(dst_pad[E + 1:].rearrange("(a b) -> a b", a=1), ends_i[:, P:P + n_pad + 1]).then_inc(edges_ready, 16)
            for tile, array in ((w_x, upd_w1[0:P, :]), (w_src, msg_w1[0:P, :]), (w_dst, msg_w1[P:2 * P, :]),
                                (w_m, upd_w1[P:2 * P, :]), (w_msg2, msg_w2), (w_out, upd_w2)):
                sp.dma_start(tile[:, :], array).then_inc(weights_in, 16)
            for tile, array in ((b_h, msg_b1), (b_msg2, msg_b2), (b_u, upd_b1)):
                with nc.allow_non_contiguous_dma(reason="one bias in a partition"):
                    sp.dma_start(tile[:, :], array.rearrange("(p a) -> p a", a=1)).then_inc(weights_in, 16)
            sp.dma_start(b_row[:, 0, :], upd_b2.rearrange("(a f) -> a f", a=1)).then_inc(weights_in, 16)
            sp.wait_ge(edges_ready, 16 * 5)
            load_edges(0, 0)
            load_x(0, 1)
            load_edges(0, 1)
            sp.wait_ge(split_made, 3)
            for k in range(3):
                sp.dma_start(b_parts[k:k + 1, :], b_split[:, k, :, :].rearrange("a q f -> a (q f)")).then_inc(parts_in, 16)
            for r in range(2, PEEL):
                load_x(0, r)
                load_edges(0, r)
            store(0, 0)
            with sp.Fori(0, LOOPS) as i:
                for r in range(PEEL, PEEL + RING):
                    load_x(i, r)
                    load_edges(i, r)
                    store(i, r - RING)
            for g in range(GROUPS - RING, GROUPS):
                store(0, g)
            for q in range(RING):
                sp.wait_ge(z_stored[q], stores_of(q))

        @block.tensor
        def _(pe):
            def turn(i, r, what):
                g, q = RING * i + r, r % RING
                order, bank = N_TURNS * g + TURNS[what], TURNS[what] % 2
                rows = {"src": src_x, "dst": dst_x}.get(what, node_x)
                first = 0 if what in ("src", "dst") else QUAD * what
                if what == "src":
                    pe.wait_ge(src_gathered[q], 16 * QUAD * use(i, r))
                elif what == "dst":
                    pe.wait_ge(dst_gathered[q], 16 * QUAD * use(i, r))
                elif what == 0:
                    pe.wait_ge(x_in[q], 16 * use(i, r))
                wait(pe, turn_copied, order - 1)
                for j in range(QUAD):
                    t = pe.transpose(turned_ps[:, bank, j * P:(j + 1) * P], rows[:, q, first + j, :], ident[:, :])
                t.then_inc(turned, 1)

            def node_pre(i, r, k):
                g = RING * i + r
                pe.wait_ge(turn_copied, N_TURNS * g + TURNS[k] + 1)
                wait(pe, u_done, NQ * g + k - 1)
                pe.matmul(pre_ps[:, k % 2, :], w_x[:, :], node_xT[:, k % 2, :], start=True, stop=True).then_inc(pre_done, 1)

            def rows_out(i, r, what):
                g = RING * i + r
                order, bank = N_OUTS * g + OUTS[what], (r * N_OUTS + OUTS[what]) % 2
                wait(pe, z_done, order - 1)
                pe.matmul(out_ps[:, bank, :], ones[:, :], b_parts[:, :], start=True, stop=False, skip_group_check=True)
                if what == "edge":
                    pe.wait_ge(edge_u_done, g + 1)
                    u = edge_u
                else:
                    pe.wait_ge(u_done, NQ * g + what + 1)
                    u = node_u[:, what % 2, :]
                for j in range(QUAD):
                    y = pe.matmul(out_ps[:, bank, j * P:(j + 1) * P], u[:, j * P:(j + 1) * P], w_out[:, :],
                                  start=False, stop=(j == QUAD - 1), skip_group_check=True)
                y.then_inc(out_done, 1)

            def group(i, r):
                g = RING * i + r
                before = (i, r - 1)
                turn(i, r, 0)
                if r:
                    rows_out(*before, 3)
                turn(i, r, 1)
                node_pre(i, r, 0)
                if r:
                    rows_out(*before, "edge")
                turn(i, r, "src")
                turn(i, r, "dst")
                node_pre(i, r, 1)
                rows_out(i, r, 0)
                pe.wait_ge(turn_copied, N_TURNS * g + TURNS["dst"] + 1)
                wait(pe, edge_pre_done, g)
                pe.matmul(edge_ps[:, 0, :], w_src[:, :], src_xT[:, :], start=True, stop=False)
                pe.matmul(edge_ps[:, 0, :], w_dst[:, :], dst_xT[:, :], start=False, stop=True).then_inc(h_pre, 1)
                turn(i, r, 2)
                rows_out(i, r, 1)
                node_pre(i, r, 2)
                pe.wait_ge(h_done, g + 1)
                wait(pe, m_done, g)
                pe.matmul(edge_ps[:, 1, :], w_fold[:, :], edge_h[:, :], start=True, stop=True).then_inc(m_pre, 1)
                turn(i, r, 3)
                rows_out(i, r, 2)
                node_pre(i, r, 3)
                pe.matmul(edge_ps[:, 0, :], w_x[:, :], dst_xT[:, :], start=True, stop=True).then_inc(edge_pre_ps, 1)

            pe.wait_ge(ident_made, 2)
            pe.wait_ge(weights_in, 16 * 10)
            pe.transpose(edge_ps[:, 0, 0:P], w_msg2[:, :], ident[:, :]).then_inc(set_pe, 1)
            pe.wait_ge(set_act, 1)
            pe.matmul(edge_ps[:, 1, 0:P], w_msg2T[:, :], w_m[:, :], start=True, stop=True)
            pe.matmul(edge_ps[:, 1, P:P + 1], w_m[:, :], b_msg2[:, :], start=True, stop=True).then_inc(set_pe, 1)
            pe.wait_ge(set_act, 3)
            pe.wait_ge(consts_made, 2)
            pe.wait_ge(parts_in, 16 * 3)
            all_groups(pe, group)
            rows_out(0, GROUPS - 1, 3)
            rows_out(0, GROUPS - 1, "edge")

        @block.scalar
        def _(act):
            def copy_turned(i, r, what):
                g = RING * i + r
                order, bank = N_TURNS * g + TURNS[what], TURNS[what] % 2
                act.wait_ge(turned, order + 1)
                if what == "src":
                    wait(act, h_pre, g)
                    to = src_xT[:, :]
                elif what == "dst":
                    wait(act, edge_pre_ps, g)
                    to = dst_xT[:, :]
                else:
                    wait(act, pre_done, NQ * g + what - 1)
                    to = node_xT[:, what % 2, :]
                act.activation(to, turned_ps[:, bank, :], ACT.Copy).then_inc(turn_copied, 1)

            def node_relu(i, r, k):
                g = RING * i + r
                act.wait_ge(pre_done, NQ * g + k + 1)
                wait(act, out_done, N_OUTS * g + OUTS[k - 2] + 1 if k >= 2 else N_OUTS * (g - 1) + OUTS[k + 2] + 1)
                act.activation(node_u[:, k % 2, :], pre_ps[:, k % 2, :], ACT.Relu, bias=b_u[:, :]).then_inc(u_done, 1)

            def edge_relu(i, r):
                g = RING * i + r
                act.wait_ge(edge_pre_done, g + 1)
                wait(act, out_done, N_OUTS * (g - 1) + OUTS["edge"] + 1)
                act.activation(edge_u[:, :], edge_pre[:, :], ACT.Relu, bias=b_u[:, :]).then_inc(edge_u_done, 1)

            def deviation(i, r):
                g = RING * i + r
                act.wait_ge(var_done, g + 1)
                wait(act, scale_done, g)
                act.activation(std[:, :], var[:, :], ACT.Sqrt, bias=eps[:, :], scale=1.0 / P).then_inc(std_done, 1)

            def normalise(i, r, blocks, last=False):
                g, q = RING * i + r, r % RING
                act.wait_ge(shift_done, g + 1)
                for b in blocks:
                    z = block_of(q, b)
                    n = act.activation(z, z, ACT.Identity, bias=shift[:, b:b + 1], scale=scale[:, b:b + 1])
                if last:
                    n.then_inc(act_normed, 1)

            def group(i, r):
                g = RING * i + r
                before = (i, r - 1)
                copy_turned(i, r, 0)
                copy_turned(i, r, 1)
                if r:
                    edge_relu(*before)
                node_relu(i, r, 0)
                copy_turned(i, r, "src")
                copy_turned(i, r, "dst")
                node_relu(i, r, 1)
                if r:
                    deviation(*before)
                act.wait_ge(h_pre, g + 1)
                wait(act, m_pre, g)
                act.activation(edge_h[:, :].rearrange("f (p j) -> f j p", j=QUAD),
                               edge_ps[:, 0, :].rearrange("f (j p) -> f j p", j=QUAD), ACT.Relu,
                               bias=b_h[:, :]).then_inc(h_done, 1)
                copy_turned(i, r, 2)
                if r:
                    normalise(*before, range(0, ACT_NORM // 2))
                node_relu(i, r, 2)
                act.wait_ge(m_pre, g + 1)
                wait(act, sum_done, g)
                act.activation(edge_m[:, :], edge_ps[:, 1, :], ACT.Identity, bias=b_fold[:, :]).then_inc(m_done, 1)
                copy_turned(i, r, 3)
                if r:
                    normalise(*before, range(ACT_NORM // 2, ACT_NORM), last=True)
                node_relu(i, r, 3)

            act.wait_ge(set_pe, 1)
            act.activation(w_msg2T[:, :], edge_ps[:, 0, 0:P], ACT.Copy).then_inc(set_act, 1)
            act.wait_ge(set_pe, 2)
            act.activation(w_fold[:, :], edge_ps[:, 1, 0:P], ACT.Copy).then_inc(set_act, 1)
            act.activation(b_fold[:, :], edge_ps[:, 1, P:P + 1], ACT.Copy).then_inc(set_act, 1)
            act.wait_ge(set_act, 3)
            act.wait_ge(consts_made, 2)
            all_groups(act, group)
            edge_relu(0, GROUPS - 1)
            deviation(0, GROUPS - 1)
            normalise(0, GROUPS - 1, range(0, ACT_NORM), last=True)

        @block.vector
        def _(dve):
            def residual(i, r, what):
                g, q = RING * i + r, r % RING
                order, bank = N_OUTS * g + OUTS[what], (r * N_OUTS + OUTS[what]) % 2
                if what == "edge":
                    if not isinstance(g, int) or g >= RING:
                        dve.wait_ge(scattered[q], 16 * QUAD * (use(i, r) - 1))
                    z, rows, b0 = edge_z[:, q], dst_x[:, q], ROWS
                else:
                    if what == 0 and (not isinstance(g, int) or g >= RING):
                        dve.wait_ge(z_stored[q], 16 * (use(i, r) - 1) + 16 * (q == 0))
                    b0 = QUAD * what
                    z, rows = node_z[:, q, b0:b0 + QUAD, :], node_x[:, q, b0:b0 + QUAD, :]
                dve.wait_ge(out_done, order + 1)
                dve.tensor_tensor(z, out_ps[:, bank, :].rearrange("p (j f) -> p j f", j=QUAD), rows, ALU.add).then_inc(z_done, 1)
                dve.wait_ge(z_done, order + 1)
                for j in range(QUAD):
                    s = dve.bn_stats(stats[:, r % 2, b0 + j, :], z[:, j, :])
                s.then_inc(stats_done, 1)

            def variance(i, r):
                g = RING * i + r
                st = stats[:, r % 2]
                dve.wait_ge(stats_done, N_OUTS * (g + 1))
                dve.tensor_tensor(diff[:, :], st[:, :, 1], st[:, :, 4], ALU.subtract).then_inc(halves_done, 1)
                dve.tensor_tensor(spread[:, :], st[:, :, 2], st[:, :, 5], ALU.add).then_inc(halves_done, 1)
                wait(dve, act_normed, g)
                dve.tensor_tensor(mean2[:, :], st[:, :, 1], st[:, :, 4], ALU.add).then_inc(halves_done, 1)
                dve.wait_ge(halves_done, 3 * (g + 1))
                dve.tensor_tensor(diff2[:, :], diff[:, :], diff[:, :], ALU.mult).then_inc(square_done, 1)
                dve.wait_ge(square_done, g + 1)
                dve.scalar_tensor_tensor(var[:, :], diff2[:, :], P / 4.0, spread[:, :], ALU.mult, ALU.add).then_inc(var_done, 1)

            def scales(i, r):
                g = RING * i + r
                dve.wait_ge(std_done, g + 1)
                dve.reciprocal(scale[:, :], std[:, :]).then_inc(scale_done, 1)
                dve.wait_ge(scale_done, g + 1)
                dve.scalar_tensor_tensor(shift[:, :], mean2[:, :], -0.5, scale[:, :], ALU.mult, ALU.mult).then_inc(shift_done, 1)

            def normalise(i, r):
                g, q = RING * i + r, r % RING
                dve.wait_ge(shift_done, g + 1)
                for b in range(ACT_NORM, BLOCKS):
                    z = block_of(q, b)
                    n = dve.tensor_scalar(z, z, scale[:, b:b + 1], shift[:, b:b + 1], ALU.mult, ALU.add)
                n.then_inc(dve_normed, 1)

            def scatter_index(i, r):
                g, q = RING * i + r, r % RING
                dve.wait_ge(dst_i_in[q], 32 * use(i, r))
                dve.tensor_tensor(same_i[:, :], dst_i[:, q, 0:QUAD], dst_i[:, q, 1:], ALU.is_equal).then_inc(same_i_done, 1)
                dve.wait_ge(same_i_done, g + 1)
                dve.scalar_tensor_tensor(out_i[:, q, :], same_i[:, :], float(FAR), dst_i[:, q, 0:QUAD],
                                         ALU.mult, ALU.add).then_inc(out_i_done, 1)

            def same_as_before(i, r):
                q = r % RING
                dve.wait_ge(dst_row_in[q], 16 * use(i, r))
                dve.tensor_tensor(same[:, :], dst_row[:, q, 1:], dst_row[:, q, 0:W], ALU.is_equal).then_inc(same_done, 1)

            def sum_edges(i, r):
                g = RING * i + r
                dve.wait_ge(m_done, g + 1)
                dve.wait_ge(same_done, g + 1)
                first = isinstance(g, int) and g == 0
                wait(dve, sum_done, g)
                dve.tensor_tensor_scan(summed[:, r % 2, :], same[:, :], edge_m[:, :],
                                       0.0 if first else summed[:, (r - 1) % 2, W - 1:W],
                                       ALU.mult, ALU.add).then_inc(sum_done, 1)

            def edge_update(i, r):
                g = RING * i + r
                dve.wait_ge(edge_pre_ps, g + 1)
                dve.wait_ge(sum_done, g + 1)
                wait(dve, edge_u_done, g)
                dve.tensor_tensor(edge_pre[:, :].rearrange("f (j p) -> f j p", j=QUAD),
                                  edge_ps[:, 0, :].rearrange("f (j p) -> f j p", j=QUAD),
                                  summed[:, r % 2, :].rearrange("f (p j) -> f j p", j=QUAD),
                                  ALU.add).then_inc(edge_pre_done, 1)

            def group(i, r):
                before = (i, r - 1)
                if r:
                    residual(*before, 3)
                    residual(*before, "edge")
                    variance(*before)
                same_as_before(i, r)
                if r:
                    scatter_index(*before)
                residual(i, r, 0)
                if r:
                    scales(*before)
                residual(i, r, 1)
                if r:
                    normalise(*before)
                sum_edges(i, r)
                residual(i, r, 2)
                edge_update(i, r)

            dve.memset(eps[:, :], EPS).then_inc(consts_made, 1)
            dve.memset(ones[:, :], 1.0).then_inc(consts_made, 1)
            dve.wait_ge(weights_in, 16 * 10)
            for k in range(3):
                part = b_row[:, k:k + 1, :]
                if k:
                    dve.wait_ge(rest_made, k)
                for j in range(QUAD):
                    c = dve.tensor_copy(b_split[:, k, j:j + 1, :], part)
                c.then_inc(split_made, 1)
                if k < 2:
                    dve.wait_ge(split_made, k + 1)
                    dve.tensor_tensor(b_row[:, k + 1:k + 2, :], part, b_split[:, k, 0:1, :], ALU.subtract).then_inc(rest_made, 1)
            all_groups(dve, group)
            last = (0, GROUPS - 1)
            residual(*last, 3)
            residual(*last, "edge")
            variance(*last)
            scatter_index(*last)
            scales(*last)
            normalise(*last)

        @block.gpsimd
        def _(pool):
            def gather(i, r):
                g, q = RING * i + r, r % RING
                pool.wait_ge(src_i_in[q], 16 * use(i, r))
                wait_alone(pool, turned, N_TURNS * (g - RING) + TURNS["src"] + 1)
                for j in range(QUAD):
                    pool.indirect_dma_start(src_x[:, q, j, :], None, x[:, :],
                                            bass.IndirectOffsetOnAxis(ap=src_i[:, q, j:j + 1], axis=0),
                                            bounds_check=N - 1, oob_is_err=False).then_inc(src_gathered[q], 16)
                pool.wait_ge(dst_i_in[q], 32 * use(i, r))
                wait_alone(pool, z_done, N_OUTS * (g - RING) + OUTS["edge"] + 1)
                for j in range(QUAD):
                    pool.indirect_dma_start(dst_x[:, q, j, :], None, x[:, :],
                                            bass.IndirectOffsetOnAxis(ap=dst_i[:, q, j:j + 1], axis=0),
                                            bounds_check=N - 1, oob_is_err=False).then_inc(dst_gathered[q], 16)

            def scatter(q, rows, index, done):
                for j in range(QUAD):
                    pool.indirect_dma_start(out[:, :], bass.IndirectOffsetOnAxis(ap=index[:, j:j + 1], axis=0),
                                            rows[:, j, :], None,
                                            bounds_check=N - 1, oob_is_err=False).then_inc(done, 16)

            def edge_rows_made(g):
                wait_alone(pool, act_normed, g + 1)
                wait_alone(pool, dve_normed, g + 1)
                wait_alone(pool, out_i_done, g + 1)

            def nodes_stored(i, r):
                q = r % RING
                wait_alone(pool, z_stored[q], 16 * use(i, r) + 16 * (q == 0))

            def last_destination(g):
                return pool.value_load(dst_pad[bass.ds(EDGES * (g + 1), 1)].rearrange("(a b) -> a b", a=1))

            def scatter_if_stored(i, r):
                g, q = RING * i + r, r % RING
                edge_rows_made(g)
                nodes_stored(i, r + 1)
                with pool.If(last_destination(g) < NODES * (g + 2) - SHORT):
                    scatter(q, edge_z[:, q], out_i[:, q], scattered[q])
                with pool.Else():
                    rows = kept_rows[bass.ds(P * g, P), :].rearrange("p (j f) -> p j f", j=QUAD)
                    pool.dma_start(rows, edge_z[:, q]).then_inc(scattered[q], 16 * (QUAD - 1))
                    pool.dma_start(kept_index[bass.ds(P * g, P), :], out_i[:, q]).then_inc(scattered[q], 16)

            def group(i, r):
                gather(i, r)
                scatter_if_stored(i, r - PEEL)

            pool.memset(zeros_i[:, :], 0).then_inc(pads_made, 1)
            pool.memset(ends_i[:, 0:P], -1).then_inc(pads_made, 1)
            pool.memset(ends_i[:, P:], N).then_inc(pads_made, 1)
            pool.memset(ident[:, :], 0.0).then_inc(ident_made, 1)
            pool.wait_ge(ident_made, 1)
            pool.affine_select(ident[:, :], ident[:, :], [[-1, P]], ALU.not_equal, 1.0, base=0,
                               channel_multiplier=1).then_inc(ident_made, 1)
            for r in range(PEEL):
                gather(0, r)
            with pool.Fori(0, LOOPS) as i:
                for r in range(PEEL, PEEL + RING):
                    group(i, r)
            for g in range(GROUPS - PEEL, CHECKED):
                scatter_if_stored(0, g)
            nodes_stored(0, GROUPS - 1)
            for g in range(CHECKED, GROUPS):
                edge_rows_made(g)
                scatter(g % RING, edge_z[:, g % RING], out_i[:, g % RING], scattered[g % RING])
            for q in range(RING):
                pool.wait_ge(scattered[q], 16 * QUAD * sum(1 for g in range(GROUPS) if g % RING == q))
            with pool.Fori(0, CHECKED) as g:
                with pool.If(last_destination(g) < NODES * (g + 2) - SHORT):
                    pool.sem_inc(back_in, 32)
                    pool.sem_inc(back_out, 16 * QUAD)
                with pool.Else():
                    pool.dma_start(back_rows[:, :, :], kept_rows[bass.ds(P * g, P), :].rearrange("p (j f) -> p j f", j=QUAD)).then_inc(back_in, 16)
                    pool.dma_start(back_i[:, :], kept_index[bass.ds(P * g, P), :]).then_inc(back_in, 16)
                    wait_alone(pool, back_in, 32 * g + 32)
                    scatter(0, back_rows, back_i, back_out)
                    pool.wait_ge(back_out, 16 * QUAD * g + 16 * QUAD)
            pool.wait_ge(back_out, 16 * QUAD * CHECKED)


_INS = ["x", "src", "dst", "L0_gnn_msg_w1", "L0_gnn_msg_b1", "L0_gnn_msg_w2", "L0_gnn_msg_b2",
        "L0_gnn_upd_w1", "L0_gnn_upd_b1", "L0_gnn_upd_w2", "L0_gnn_upd_b2"]


def kernel(**inputs):
    import concourse.bacc as bacc
    from concourse.bass_utils import run_bass_kernel_spmd

    nc = bacc.Bacc("TRN2", target_bir_lowering=False, num_devices=1)
    arrays, args = {}, []
    for name in _INS:
        a = np.ascontiguousarray(inputs[name])
        arrays[f"in_{name}"] = a
        args.append(nc.dram_tensor(f"in_{name}", a.shape, mybir.dt.from_np(a.dtype), kind="ExternalInput").ap())
    shape = inputs["x"].shape
    args.append(nc.dram_tensor("out_0", shape, F32, kind="ExternalOutput").ap())
    gnn_resnorm(nc, *args)
    r = run_bass_kernel_spmd(nc, [arrays], core_ids=[0])
    return r.results[0]["out_0"]
```

```python
from contextlib import ExitStack

import numpy as np
import concourse.bass as bass
from concourse import mybir

ALU = mybir.AluOpType
ACT = mybir.ActivationFunctionType
F32 = mybir.dt.float32
BF16 = mybir.dt.bfloat16
I32 = mybir.dt.int32

P = 128
QUAD = 4
W = QUAD * P
ROWS = 16
NODES = P * ROWS
EDGES = W
NQ = ROWS // QUAD
RING = 4
PEEL = 5
EPS = 1e-5

TURNS = {0: 0, 1: 1, 2: 2, "src": 3, "dst": 4, 3: 5}
N_TURNS = len(TURNS)
OUTS = {0: 0, 1: 1, 2: 2, 3: 3, "edge": 4}
N_OUTS = len(OUTS)
BLOCKS = ROWS + QUAD
ACT_NORM = 9
ACT_FIRST, ACT_SECOND, ACT_LATE = range(0, 3), range(3, 5), range(5, ACT_NORM)
DVE_SPLIT = 3


def gnn_resnorm(nc, x, src, dst, msg_w1, msg_b1, msg_w2, msg_b2, upd_w1, upd_b1, upd_w2, upd_b2, out):
    N, D = x.shape
    E = src.shape[0]
    GROUPS = -(-N // NODES)
    SHORT = GROUPS * NODES - N
    E_PAD = GROUPS * EDGES
    assert D == P and E_PAD >= E and (GROUPS - PEEL) % RING == 0 and SHORT % ROWS == 0
    LOOPS = (GROUPS - PEEL) // RING
    COLS = E_PAD // P
    PART = E_PAD // 8
    FIRST_CHECK = 2 * NODES - SHORT
    FAR = 1 << 20
    CHECKED = GROUPS - 2
    SPLIT = 10
    assert E % SPLIT == 0 and N < FAR

    src_pad = nc.dram_tensor("src_pad", [E_PAD], I32).ap()
    dst_pad = nc.dram_tensor("dst_pad", [E_PAD + 2], I32).ap()
    goes_on = nc.dram_tensor("goes_on", [E_PAD], BF16).ap()
    pairs = nc.dram_tensor("pairs", [E_PAD, 2], I32).ap()
    kept_rows = nc.dram_tensor("kept_rows", [GROUPS * P, QUAD * P], F32).ap()
    kept_index = nc.dram_tensor("kept_index", [GROUPS * P, QUAD], I32).ap()

    with ExitStack() as ctx:
        def sb(name, shape, dt=F32):
            return ctx.enter_context(nc.sbuf_tensor(name, shape, dt))

        def sem(name):
            return ctx.enter_context(nc.semaphore(name))

        def sems(name):
            return [sem(f"{name}{q}") for q in range(RING)]

        turned_ps = ctx.enter_context(nc.psum_tensor("turned_ps", [P, 2, W], F32))
        pre_ps = ctx.enter_context(nc.psum_tensor("pre_ps", [P, 2, W], F32))
        out_ps = ctx.enter_context(nc.psum_tensor("out_ps", [P, 2, W], F32))
        edge_ps = ctx.enter_context(nc.psum_tensor("edge_ps", [P, 2, W], F32))

        w_msg1, w_upd1 = sb("w_msg1", [P, 2, P]), sb("w_upd1", [P, 2, P])
        w_src, w_dst, w_x, w_m = w_msg1[:, 0, :], w_msg1[:, 1, :], w_upd1[:, 0, :], w_upd1[:, 1, :]
        w_msg2, w_msg2T, w_fold, w_out, ident = (
            sb(n, [P, P]) for n in ("w_msg2", "w_msg2T", "w_fold", "w_out", "ident"))
        b_h, b_msg2, b_fold, b_u, eps = (sb(n, [P, 1]) for n in ("b_h", "b_msg2", "b_fold", "b_u", "eps"))
        b_row = sb("b_row", [1, 3, P])
        b_split = sb("b_split", [1, 3, QUAD, P], BF16)
        b_parts = sb("b_parts", [3, W], BF16)
        ones = sb("ones", [3, P], BF16)
        zeros_i = sb("zeros_i", [1, P], I32)
        ends_i = sb("ends_i", [1, 2 * P], I32)

        node_x = sb("node_x", [P, RING, ROWS, P])
        node_z = sb("node_z", [P, RING, ROWS, P])
        src_i = sb("src_i", [P, RING, QUAD], I32)
        dst_i = sb("dst_i", [P, RING, QUAD + 1], I32)
        same = sb("same", [P, RING, W], BF16)
        src_x = sb("src_x", [P, RING, QUAD, P])
        dst_x = sb("dst_x", [P, RING, QUAD, P])
        edge_z = sb("edge_z", [P, RING, QUAD, P])
        out_i = sb("out_i", [P, RING, QUAD], I32)
        same_i = sb("same_i", [P, QUAD], I32)

        node_xT = sb("node_xT", [P, 2, W])
        node_u = sb("node_u", [P, 2, W])
        src_xT = sb("src_xT", [P, W])
        dst_xT = sb("dst_xT", [P, W])
        edge_h = sb("edge_h", [P, W])
        edge_m = sb("edge_m", [P, W])
        summed = sb("summed", [P, 2, W])
        edge_pre = sb("edge_pre", [P, W])
        edge_u = sb("edge_u", [P, W])

        stats = sb("stats", [P, 2, BLOCKS, 6])
        mean2, diff, spread, diff2, var, std, scale, shift = (
            sb(n, [P, BLOCKS]) for n in
            ("mean2", "diff", "spread", "diff2", "var", "std", "scale", "shift"))

        all_dst, all_next, all_before = (sb(n, [P, COLS], I32) for n in ("all_dst", "all_next", "all_before"))
        all_same = sb("all_same", [P, COLS], BF16)
        ones_p = sb("ones_p", [P, 1])
        falls, falls_p = sb("falls", [P, COLS]), sb("falls_p", [P, 1])
        unsorted = sb("unsorted", [1, 1], I32)
        last_dst, checked_to, far = (sb(n, [1, GROUPS], I32) for n in ("last_dst", "checked_to", "far"))
        any_far = sb("any_far", [1, 1], I32)
        pair_in, pair_tile = sb("pair_in", [P, 2, COLS], I32), sb("pair_tile", [P, COLS, 2], I32)
        pair_col, place_col = sb("pair_col", [P, 2], I32), sb("place_col", [P, 1], I32)
        dst_f, number, places, less, equal_before = (
            sb(n, [P, COLS]) for n in ("dst_f", "number", "places", "less", "equal_before"))
        number_i, places_i = sb("number_i", [P, COLS], I32), sb("places_i", [P, COLS], I32)
        part_i, part_f = sb("part_i", [P, PART], I32), sb("part_f", [P, PART])
        part_number_i, part_number = sb("part_number_i", [P, PART], I32), sb("part_number", [P, PART])
        part_hits, part_before = sb("part_hits", [P, PART], BF16), sb("part_before", [P, PART], BF16)

        back_rows = sb("back_rows", [P, QUAD, P])
        back_i = sb("back_i", [P, QUAD], I32)

        weights_in = sem("weights_in")
        more_weights_in, before_in = sem("more_weights_in"), sem("before_in")
        waits_passed = sem("waits_passed")
        ident_made, pads_made, edges_ready = (sem(n) for n in ("ident_made", "pads_made", "edges_ready"))
        consts_made, split_made, rest_made, parts_in = (
            sem(n) for n in ("consts_made", "split_made", "rest_made", "parts_in"))
        set_pe, set_act = sem("set_pe"), sem("set_act")
        x_in, z_stored = sems("x_in"), sems("z_stored")
        src_i_in, dst_i_in, same_in = sems("src_i_in"), sems("dst_i_in"), sems("same_in")
        all_in, falls_made, falls_max, falls_added, unsorted_made = (
            sem(n) for n in ("all_in", "falls_made", "falls_max", "falls_added", "unsorted_made"))
        numbers_made, part_in, part_ready, compared, counted, places_made, placed = (
            sem(n) for n in ("numbers_made", "part_in", "part_ready", "compared", "counted", "places_made", "placed"))
        dst_f_made, number_moved, pair_loaded, col_made, apart, rewritten = (
            sem(n) for n in ("dst_f_made", "number_moved", "pair_loaded", "col_made", "apart", "rewritten"))
        in_order, all_same_made, goes_on_out = (sem(n) for n in ("in_order", "all_same_made", "goes_on_out"))
        checks_made, last_dst_in, far_made, any_far_made = (
            sem(n) for n in ("checks_made", "last_dst_in", "far_made", "any_far_made"))
        src_gathered, dst_gathered, scattered = sems("src_gathered"), sems("dst_gathered"), sems("scattered")
        turned, turn_copied = sem("turned"), sem("turn_copied")
        pre_done, u_done = sem("pre_done"), sem("u_done")
        out_done, z_done, stats_done = sem("out_done"), sem("z_done"), sem("stats_done")
        h_pre, h_done, m_pre, m_done = (sem(n) for n in ("h_pre", "h_done", "m_pre", "m_done"))
        sum_done, edge_pre_ps, edge_pre_done, edge_u_done = (
            sem(n) for n in ("sum_done", "edge_pre_ps", "edge_pre_done", "edge_u_done"))
        same_i_done, out_i_done = sem("same_i_done"), sem("out_i_done")
        halves_done, square_done, var_done, std_done, scale_done, shift_done = (
            sem(n) for n in ("halves_done", "square_done", "var_done", "std_done", "scale_done", "shift_done"))
        act_normed, dve_normed = sem("act_normed"), sem("dve_normed")
        back_in, back_out = sem("back_in"), sem("back_out")

        def first_node(g):
            return 0 if isinstance(g, int) and g == 0 else NODES * g - SHORT

        def use(i, r):
            return i + r // RING + 1

        def wait(eng, s, value):
            if not isinstance(value, int) or value > 0:
                eng.wait_ge(s, value)

        def wait_alone(eng, s, value):
            wait(eng, s, value)
            if not isinstance(value, int):
                eng.sem_inc(waits_passed, 1)

        def all_groups(eng, group):
            for r in range(PEEL):
                group(0, r)
            with eng.Fori(0, LOOPS) as i:
                for r in range(PEEL, PEEL + RING):
                    group(i, r)

        def block_of(q, b):
            return node_z[:, q, b, :] if b < ROWS else edge_z[:, q, b - ROWS, :]

        def whole(a):
            return a.rearrange("(p c) -> p c", p=P)

        def stores_of(q):
            return 16 * sum(1 for g in range(GROUPS) if g % RING == q) + 16 * (q == 0)

        block = ctx.enter_context(nc.Block())

        @block.sync
        def _(sp):
            def load_x(i, r):
                g, q = RING * i + r, r % RING
                wait(sp, z_done, N_OUTS * (g - RING) + OUTS[3] + 1)
                rows = x[bass.ds(first_node(g), NODES), :].rearrange("(p j) f -> p j f", j=ROWS)
                sp.dma_start(node_x[:, q], rows).then_inc(x_in[q], 16)

            def load_edges(i, r):
                load_ends(i, r)
                load_same(i, r)

            def load_ends(i, r):
                g, q = RING * i + r, r % RING
                if not isinstance(g, int) or g >= RING:
                    wait_alone(sp, src_gathered[q], 16 * QUAD * (use(i, r) - 1))
                    wait_alone(sp, dst_gathered[q], 16 * QUAD * (use(i, r) - 1))
                    sp.wait_ge(out_i_done, g - RING + 1)
                s = src_pad[bass.ds(EDGES * g, EDGES)].rearrange("(p j) -> p j", j=QUAD)
                sp.dma_start(src_i[:, q, :], s).then_inc(src_i_in[q], 16)
                d = dst_pad[bass.ds(EDGES * g + 1, EDGES)]
                d = bass.AP(d.tensor, d.offset, [[QUAD, P], [1, QUAD + 1]])
                sp.dma_start(dst_i[:, q, :], d).then_inc(dst_i_in[q], 16)

            def load_same(i, r):
                g, q = RING * i + r, r % RING
                wait_alone(sp, sum_done, g - RING + 1)
                row = goes_on[bass.ds(EDGES * g, EDGES)].rearrange("(a w) -> a w", a=1).partition_broadcast(P)
                sp.dma_start(same[:, q, :], row).then_inc(same_in[q], 16)

            def store(i, r):
                g, q = RING * i + r, r % RING
                sp.wait_ge(act_normed, g + 1)
                sp.wait_ge(dve_normed, g + 1)
                if isinstance(g, int) and g == 0:
                    full = (NODES - SHORT) // ROWS
                    for a, b in ((0, full // 8 * 8), (full // 8 * 8, full)):
                        rows = out[a * ROWS:b * ROWS, :].rearrange("(p j) f -> p j f", j=ROWS)
                        sp.dma_start(rows, node_z[a:b, q]).then_inc(z_stored[q], 16)
                    return
                rows = out[bass.ds(first_node(g), NODES), :].rearrange("(p j) f -> p j f", j=ROWS)
                sp.dma_start(rows, node_z[:, q]).then_inc(z_stored[q], 16)

            def lists(name):
                return name.rearrange("(a b) -> a b", a=SPLIT)

            sp.dma_start(lists(dst_pad[1:E + 1]), lists(dst)).then_inc(edges_ready, 16)
            sp.dma_start(lists(src_pad[0:E]), lists(src)).then_inc(edges_ready, 16)
            sp.wait_ge(pads_made, 3)
            n_pad = E_PAD - E
            sp.dma_start(dst_pad[0:1].rearrange("(a b) -> a b", a=1), ends_i[:, 0:1]).then_inc(edges_ready, 16)
            sp.dma_start(dst_pad[E + 1:].rearrange("(a b) -> a b", a=1), ends_i[:, P:P + n_pad + 1]).then_inc(edges_ready, 16)
            sp.dma_start(src_pad[E:E_PAD].rearrange("(a b) -> a b", a=1), zeros_i[:, 0:n_pad]).then_inc(edges_ready, 16)
            load_x(0, 0)
            halves = "(k p) f -> p k f"
            sp.dma_start(w_upd1[:, :, :], upd_w1.rearrange(halves, p=P)).then_inc(weights_in, 16)
            sp.wait_ge(edges_ready, 16 * 5)
            for tile, first in ((all_dst, 1), (all_next, 2)):
                sp.dma_start(tile[:, :], whole(dst_pad[first:first + E_PAD])).then_inc(all_in, 16)
            with nc.allow_non_contiguous_dma(reason="one bias in a partition"):
                sp.dma_start(b_u[:, :], upd_b1.rearrange("(p a) -> p a", a=1)).then_inc(weights_in, 16)
            sp.dma_start(b_row[:, 0, :], upd_b2.rearrange("(a f) -> a f", a=1)).then_inc(weights_in, 16)
            sp.dma_start(w_out[:, :], upd_w2).then_inc(weights_in, 16)
            sp.dma_start(w_msg1[:, :, :], msg_w1.rearrange(halves, p=P)).then_inc(more_weights_in, 16)
            sp.dma_start(w_msg2[:, :], msg_w2).then_inc(more_weights_in, 16)
            for tile, array in ((b_h, msg_b1), (b_msg2, msg_b2)):
                with nc.allow_non_contiguous_dma(reason="one bias in a partition"):
                    sp.dma_start(tile[:, :], array.rearrange("(p a) -> p a", a=1)).then_inc(more_weights_in, 16)
            sp.wait_ge(in_order, 1)
            load_ends(0, 0)
            sp.dma_start(all_before[:, :], whole(dst_pad[0:E_PAD])).then_inc(before_in, 16)
            sp.wait_ge(split_made, 3)
            for k in range(3):
                sp.dma_start(b_parts[k:k + 1, :], b_split[:, k, :, :].rearrange("a q f -> a (q f)")).then_inc(parts_in, 16)
            load_ends(0, 1)
            load_x(0, 1)
            sp.wait_ge(all_same_made, 1)
            sp.dma_start(whole(goes_on), all_same[:, :]).then_inc(goes_on_out, 16)
            with nc.allow_non_contiguous_dma(reason="one destination a group"):
                sp.dma_start(last_dst[:, :], dst_pad[1:E_PAD + 1].rearrange("(a g w) -> a g w", a=1, w=EDGES)[:, :, EDGES - 1]).then_inc(last_dst_in, 16)
            sp.wait_ge(goes_on_out, 16)
            load_same(0, 0)
            load_same(0, 1)
            for r in range(2, PEEL):
                sp.wait_ge(dst_gathered[r - 2], 16 * QUAD)
                load_x(0, r)
                load_edges(0, r)
            store(0, 0)
            with sp.Fori(0, LOOPS) as i:
                for r in range(PEEL, PEEL + RING):
                    load_x(i, r)
                    load_edges(i, r)
                    store(i, r - RING)
            for g in range(GROUPS - RING, GROUPS):
                store(0, g)
            for q in range(RING):
                sp.wait_ge(z_stored[q], stores_of(q))

        @block.tensor
        def _(pe):
            def turn(i, r, what):
                g, q = RING * i + r, r % RING
                order, bank = N_TURNS * g + TURNS[what], TURNS[what] % 2
                rows = {"src": src_x, "dst": dst_x}.get(what, node_x)
                first = 0 if what in ("src", "dst") else QUAD * what
                if what == "src":
                    pe.wait_ge(src_gathered[q], 16 * QUAD * use(i, r))
                elif what == "dst":
                    pe.wait_ge(dst_gathered[q], 16 * QUAD * use(i, r))
                elif what == 0:
                    pe.wait_ge(x_in[q], 16 * use(i, r))
                wait(pe, turn_copied, order - 1)
                for j in range(QUAD):
                    t = pe.transpose(turned_ps[:, bank, j * P:(j + 1) * P], rows[:, q, first + j, :], ident[:, :])
                t.then_inc(turned, 1)

            def node_pre(i, r, k):
                g = RING * i + r
                pe.wait_ge(turn_copied, N_TURNS * g + TURNS[k] + 1)
                wait(pe, u_done, NQ * g + k - 1)
                pe.matmul(pre_ps[:, k % 2, :], w_x, node_xT[:, k % 2, :], start=True, stop=True).then_inc(pre_done, 1)

            def rows_out(i, r, what):
                g = RING * i + r
                order, bank = N_OUTS * g + OUTS[what], (r * N_OUTS + OUTS[what]) % 2
                wait(pe, z_done, order - 1)
                pe.matmul(out_ps[:, bank, :], ones[:, :], b_parts[:, :], start=True, stop=False, skip_group_check=True)
                if what == "edge":
                    pe.wait_ge(edge_u_done, g + 1)
                    u = edge_u
                else:
                    pe.wait_ge(u_done, NQ * g + what + 1)
                    u = node_u[:, what % 2, :]
                for j in range(QUAD):
                    y = pe.matmul(out_ps[:, bank, j * P:(j + 1) * P], u[:, j * P:(j + 1) * P], w_out[:, :],
                                  start=False, stop=(j == QUAD - 1), skip_group_check=True)
                y.then_inc(out_done, 1)

            def ends_pre(i, r):
                g = RING * i + r
                pe.wait_ge(turn_copied, N_TURNS * g + TURNS["dst"] + 1)
                wait(pe, edge_pre_done, g)
                pe.matmul(edge_ps[:, 0, :], w_src, src_xT[:, :], start=True, stop=False)
                pe.matmul(edge_ps[:, 0, :], w_dst, dst_xT[:, :], start=False, stop=True).then_inc(h_pre, 1)

            def message(i, r):
                g = RING * i + r
                pe.wait_ge(h_done, g + 1)
                wait(pe, m_done, g)
                pe.matmul(edge_ps[:, 1, :], w_fold[:, :], edge_h[:, :], start=True, stop=True).then_inc(m_pre, 1)

            def destination_pre(i, r):
                pe.matmul(edge_ps[:, 0, :], w_x, dst_xT[:, :], start=True, stop=True).then_inc(edge_pre_ps, 1)

            def group(i, r):
                before = (i, r - 1)
                turn(i, r, 0)
                if r:
                    rows_out(*before, 3)
                turn(i, r, 1)
                node_pre(i, r, 0)
                turn(i, r, 2)
                if r:
                    rows_out(*before, "edge")
                node_pre(i, r, 1)
                rows_out(i, r, 0)
                turn(i, r, "src")
                turn(i, r, "dst")
                node_pre(i, r, 2)
                rows_out(i, r, 1)
                ends_pre(i, r)
                turn(i, r, 3)
                rows_out(i, r, 2)
                message(i, r)
                node_pre(i, r, 3)
                destination_pre(i, r)

            pe.wait_ge(falls_max, 1)
            pe.wait_ge(numbers_made, 1)
            pe.matmul(out_ps[0:1, 1, 0:1], falls_p[:, :], ones_p[:, :], start=True, stop=True).then_inc(falls_added, 1)
            pe.wait_ge(ident_made, 2)
            pe.wait_ge(weights_in, 16 * 4)
            pe.wait_ge(more_weights_in, 16 * 4)
            pe.transpose(edge_ps[:, 0, 0:P], w_msg2[:, :], ident[:, :]).then_inc(set_pe, 1)
            pe.wait_ge(set_act, 1)
            pe.matmul(edge_ps[:, 1, 0:P], w_msg2T[:, :], w_m, start=True, stop=True)
            pe.matmul(edge_ps[:, 1, P:P + 1], w_m, b_msg2[:, :], start=True, stop=True).then_inc(set_pe, 1)
            pe.wait_ge(set_act, 3)
            pe.wait_ge(consts_made, 2)
            pe.wait_ge(unsorted_made, 1)
            pe.wait_ge(parts_in, 16 * 3)
            all_groups(pe, group)
            rows_out(0, GROUPS - 1, 3)
            rows_out(0, GROUPS - 1, "edge")

        @block.scalar
        def _(act):
            def copy_turned(i, r, what):
                g = RING * i + r
                order, bank = N_TURNS * g + TURNS[what], TURNS[what] % 2
                act.wait_ge(turned, order + 1)
                if what == "src":
                    wait(act, h_pre, g)
                    to = src_xT[:, :]
                elif what == "dst":
                    wait(act, edge_pre_ps, g)
                    to = dst_xT[:, :]
                else:
                    wait(act, pre_done, NQ * g + what - 1)
                    to = node_xT[:, what % 2, :]
                act.activation(to, turned_ps[:, bank, :], ACT.Copy).then_inc(turn_copied, 1)

            def node_relu(i, r, k):
                g = RING * i + r
                act.wait_ge(pre_done, NQ * g + k + 1)
                wait(act, out_done, N_OUTS * g + OUTS[k - 2] + 1 if k >= 2 else N_OUTS * (g - 1) + OUTS[k + 2] + 1)
                act.activation(node_u[:, k % 2, :], pre_ps[:, k % 2, :], ACT.Relu, bias=b_u[:, :]).then_inc(u_done, 1)

            def edge_relu(i, r):
                g = RING * i + r
                act.wait_ge(edge_pre_done, g + 1)
                wait(act, out_done, N_OUTS * (g - 1) + OUTS["edge"] + 1)
                act.activation(edge_u[:, :], edge_pre[:, :], ACT.Relu, bias=b_u[:, :]).then_inc(edge_u_done, 1)

            def deviation(i, r):
                g = RING * i + r
                act.wait_ge(var_done, g + 1)
                wait(act, scale_done, g)
                act.activation(std[:, :], var[:, :], ACT.Sqrt, bias=eps[:, :], scale=1.0 / P).then_inc(std_done, 1)

            def normalise(i, r, blocks, last=False):
                g, q = RING * i + r, r % RING
                act.wait_ge(shift_done, g + 1)
                for b in blocks:
                    z = block_of(q, b)
                    n = act.activation(z, z, ACT.Identity, bias=shift[:, b:b + 1], scale=scale[:, b:b + 1])
                if last:
                    n.then_inc(act_normed, 1)

            def ends_relu(i, r):
                g = RING * i + r
                act.wait_ge(h_pre, g + 1)
                wait(act, m_pre, g)
                act.activation(edge_h[:, :].rearrange("f (p j) -> f j p", j=QUAD),
                               edge_ps[:, 0, :].rearrange("f (j p) -> f j p", j=QUAD), ACT.Relu,
                               bias=b_h[:, :]).then_inc(h_done, 1)

            def message_bias(i, r):
                g = RING * i + r
                act.wait_ge(m_pre, g + 1)
                wait(act, sum_done, g)
                act.activation(edge_m[:, :], edge_ps[:, 1, :], ACT.Identity, bias=b_fold[:, :]).then_inc(m_done, 1)

            def group(i, r):
                before = (i, r - 1)
                copy_turned(i, r, 0)
                if r:
                    edge_relu(*before)
                copy_turned(i, r, 1)
                node_relu(i, r, 0)
                copy_turned(i, r, 2)
                if r > 1:
                    normalise(i, r - 2, ACT_LATE, last=True)
                node_relu(i, r, 1)
                copy_turned(i, r, "src")
                copy_turned(i, r, "dst")
                node_relu(i, r, 2)
                if r:
                    deviation(*before)
                    normalise(*before, ACT_FIRST)
                ends_relu(i, r)
                copy_turned(i, r, 3)
                if r:
                    normalise(*before, ACT_SECOND)
                message_bias(i, r)
                node_relu(i, r, 3)

            act.wait_ge(set_pe, 1)
            act.activation(w_msg2T[:, :], edge_ps[:, 0, 0:P], ACT.Copy).then_inc(set_act, 1)
            act.wait_ge(set_pe, 2)
            act.activation(w_fold[:, :], edge_ps[:, 1, 0:P], ACT.Copy).then_inc(set_act, 1)
            act.activation(b_fold[:, :], edge_ps[:, 1, P:P + 1], ACT.Copy).then_inc(set_act, 1)
            act.wait_ge(set_act, 3)
            act.wait_ge(consts_made, 2)
            all_groups(act, group)
            edge_relu(0, GROUPS - 1)
            normalise(0, GROUPS - 2, ACT_LATE, last=True)
            deviation(0, GROUPS - 1)
            normalise(0, GROUPS - 1, range(0, ACT_NORM), last=True)

        @block.vector
        def _(dve):
            def residual(i, r, what, between=lambda: None):
                g, q = RING * i + r, r % RING
                order, bank = N_OUTS * g + OUTS[what], (r * N_OUTS + OUTS[what]) % 2
                if what == "edge":
                    if not isinstance(g, int) or g >= RING:
                        dve.wait_ge(scattered[q], 16 * QUAD * (use(i, r) - 1))
                    z, rows, b0 = edge_z[:, q], dst_x[:, q], ROWS
                else:
                    if what == 0 and (not isinstance(g, int) or g >= RING):
                        dve.wait_ge(z_stored[q], 16 * (use(i, r) - 1) + 16 * (q == 0))
                    b0 = QUAD * what
                    z, rows = node_z[:, q, b0:b0 + QUAD, :], node_x[:, q, b0:b0 + QUAD, :]
                dve.wait_ge(out_done, order + 1)
                dve.tensor_tensor(z, out_ps[:, bank, :].rearrange("p (j f) -> p j f", j=QUAD), rows, ALU.add).then_inc(z_done, 1)
                between()
                dve.wait_ge(z_done, order + 1)
                for j in range(QUAD):
                    s = dve.bn_stats(stats[:, r % 2, b0 + j, :], z[:, j, :])
                s.then_inc(stats_done, 1)

            def variance(i, r, between=lambda: None):
                g = RING * i + r
                st = stats[:, r % 2]
                dve.wait_ge(stats_done, N_OUTS * (g + 1))
                dve.tensor_tensor(diff[:, :], st[:, :, 1], st[:, :, 4], ALU.subtract).then_inc(halves_done, 1)
                dve.tensor_tensor(spread[:, :], st[:, :, 2], st[:, :, 5], ALU.add).then_inc(halves_done, 1)
                wait(dve, act_normed, g)
                dve.tensor_tensor(mean2[:, :], st[:, :, 1], st[:, :, 4], ALU.add).then_inc(halves_done, 1)
                between()
                dve.wait_ge(halves_done, 3 * (g + 1))
                dve.tensor_tensor(diff2[:, :], diff[:, :], diff[:, :], ALU.mult).then_inc(square_done, 1)
                dve.wait_ge(square_done, g + 1)
                dve.scalar_tensor_tensor(var[:, :], diff2[:, :], P / 4.0, spread[:, :], ALU.mult, ALU.add).then_inc(var_done, 1)

            def scales(i, r):
                g = RING * i + r
                dve.wait_ge(std_done, g + 1)
                dve.reciprocal(scale[:, :], std[:, :]).then_inc(scale_done, 1)
                dve.wait_ge(scale_done, g + 1)
                dve.scalar_tensor_tensor(shift[:, :], mean2[:, :], -0.5, scale[:, :], ALU.mult, ALU.mult).then_inc(shift_done, 1)

            def normalise(i, r, blocks, last=False):
                g, q = RING * i + r, r % RING
                dve.wait_ge(shift_done, g + 1)
                for b in blocks:
                    z = block_of(q, b)
                    n = dve.tensor_scalar(z, z, scale[:, b:b + 1], shift[:, b:b + 1], ALU.mult, ALU.add)
                if last:
                    n.then_inc(dve_normed, 1)

            def same_as_next(i, r):
                g, q = RING * i + r, r % RING
                dve.wait_ge(dst_i_in[q], 16 * use(i, r))
                dve.tensor_tensor(same_i[:, :], dst_i[:, q, 0:QUAD], dst_i[:, q, 1:], ALU.is_equal).then_inc(same_i_done, 1)

            def scatter_index(i, r):
                g, q = RING * i + r, r % RING
                dve.wait_ge(same_i_done, g + 1)
                dve.scalar_tensor_tensor(out_i[:, q, :], same_i[:, :], float(FAR), dst_i[:, q, 0:QUAD],
                                         ALU.mult, ALU.add).then_inc(out_i_done, 1)

            def sum_edges(i, r):
                g = RING * i + r
                dve.wait_ge(m_done, g + 1)
                dve.wait_ge(same_in[r % RING], 16 * use(i, r))
                first = isinstance(g, int) and g == 0
                wait(dve, sum_done, g)
                dve.tensor_tensor_scan(summed[:, r % 2, :], same[:, r % RING, :], edge_m[:, :],
                                       0.0 if first else summed[:, (r - 1) % 2, W - 1:W],
                                       ALU.mult, ALU.add).then_inc(sum_done, 1)

            def edge_update(i, r):
                g = RING * i + r
                dve.wait_ge(edge_pre_ps, g + 1)
                dve.wait_ge(sum_done, g + 1)
                wait(dve, edge_u_done, g)
                dve.tensor_tensor(edge_pre[:, :].rearrange("f (j p) -> f j p", j=QUAD),
                                  edge_ps[:, 0, :].rearrange("f (j p) -> f j p", j=QUAD),
                                  summed[:, r % 2, :].rearrange("f (p j) -> f j p", j=QUAD),
                                  ALU.add).then_inc(edge_pre_done, 1)

            def group(i, r):
                if not r:
                    residual(i, r, 0)
                    residual(i, r, 1)
                    residual(i, r, 2)
                    sum_edges(i, r)
                    edge_update(i, r)
                    return
                before = (i, r - 1)
                part = [range(ACT_NORM + DVE_SPLIT * k, ACT_NORM + DVE_SPLIT * (k + 1)) for k in range(2)]
                residual(*before, 3)
                residual(*before, "edge", lambda: same_as_next(*before))
                variance(*before, lambda: scatter_index(*before))
                residual(i, r, 0)
                scales(*before)
                residual(i, r, 1, lambda: normalise(*before, part[0]))
                residual(i, r, 2, lambda: normalise(*before, part[1]))
                sum_edges(i, r)
                edge_update(i, r)
                normalise(*before, range(part[1].stop, BLOCKS), last=True)

            def order_edges():
                dve.memset(ones_p[:, :], 1.0).then_inc(numbers_made, 1)
                dve.wait_ge(all_in, 16 * 2)
                dve.tensor_tensor(falls[:, :], all_dst[:, :], all_next[:, :], ALU.is_gt).then_inc(falls_made, 1)
                dve.wait_ge(falls_made, 1)
                dve.tensor_reduce(falls_p[:, :], falls[:, :], mybir.AxisListType.X, ALU.max).then_inc(falls_max, 1)
                dve.wait_ge(falls_added, 1)
                dve.tensor_copy(unsorted[:, :], out_ps[0:1, 1, 0:1]).then_inc(unsorted_made, 1)
                dve.wait_ge(unsorted_made, 1)
                with dve.If(dve.value_load(unsorted[:, :]) > 0):
                    count_places()
                with dve.Else():
                    dve.sem_inc(waits_passed, 1)

            def mark_sums():
                dve.wait_ge(in_order, 1)
                dve.wait_ge(before_in, 16)
                dve.tensor_tensor(all_same[:, :], all_dst[:, :], all_before[:, :], ALU.is_equal).then_inc(all_same_made, 1)

            def mark_far():
                dve.wait_ge(last_dst_in, 16)
                dve.wait_ge(checks_made, 1)
                dve.tensor_tensor(far[:, :], last_dst[:, :], checked_to[:, :], ALU.is_ge).then_inc(far_made, 1)
                dve.wait_ge(far_made, 1)
                dve.tensor_reduce(any_far[:, :], far[:, 0:CHECKED], mybir.AxisListType.X, ALU.max).then_inc(any_far_made, 1)

            def count_places():
                dve.wait_ge(checks_made, 3)
                dve.tensor_copy(dst_f[:, :], all_dst[:, :]).then_inc(dst_f_made, 1)
                dve.tensor_copy(number[:, :], number_i[:, :]).then_inc(dst_f_made, 1)
                dve.tensor_copy(part_number[:, :], part_number_i[:, :]).then_inc(dst_f_made, 1)
                dve.memset(places[:, :], 0.0).then_inc(dst_f_made, 1)
                dve.wait_ge(dst_f_made, 4)
                with dve.Fori(0, E_PAD // PART) as part:
                    dve.wait_ge(part_in, 16 * part + 16)
                    dve.tensor_copy(part_f[:, :], part_i[:, :]).then_inc(part_ready, 1)
                    wait_alone(dve, part_ready, part + 1)
                    with dve.Fori(0, COLS) as c:
                        edge, at = dst_f[:, bass.ds(c, 1)], number[:, bass.ds(c, 1)]
                        dve.tensor_scalar(part_hits[:, :], part_f[:, :], edge, None, ALU.is_lt, ALU.add,
                                          accum_out=less[:, bass.ds(c, 1)]).then_inc(compared, 1)
                        dve.tensor_scalar(part_before[:, :], part_number[:, :], at, None, ALU.is_lt).then_inc(compared, 1)
                        dve.wait_ge(compared, part * (3 * COLS) + 3 * c + 2)
                        dve.scalar_tensor_tensor(part_hits[:, :], part_f[:, :], edge, part_before[:, :], ALU.is_equal,
                                                 ALU.mult, accum_out=equal_before[:, bass.ds(c, 1)]).then_inc(compared, 1)
                        dve.wait_ge(compared, part * (3 * COLS) + 3 * c + 3)
                    dve.tensor_tensor(places[:, :], places[:, :], less[:, :], ALU.add).then_inc(counted, 1)
                    dve.wait_ge(counted, part * 3 + 1)
                    dve.tensor_tensor(places[:, :], places[:, :], equal_before[:, :], ALU.add).then_inc(counted, 1)
                    dve.tensor_scalar(number[:, :], number[:, :], float(-PART), None, ALU.add).then_inc(counted, 1)
                    dve.wait_ge(counted, part * 3 + 3)
                dve.tensor_copy(places_i[:, :], places[:, :]).then_inc(placed, 1)

            dve.memset(eps[:, :], EPS).then_inc(consts_made, 1)
            dve.memset(ones[:, :], 1.0).then_inc(consts_made, 1)
            order_edges()
            dve.wait_ge(weights_in, 16 * 4)
            for k in range(3):
                part = b_row[:, k:k + 1, :]
                if k:
                    dve.wait_ge(rest_made, k)
                for j in range(QUAD):
                    c = dve.tensor_copy(b_split[:, k, j:j + 1, :], part)
                c.then_inc(split_made, 1)
                if k < 2:
                    dve.wait_ge(split_made, k + 1)
                    dve.tensor_tensor(b_row[:, k + 1:k + 2, :], part, b_split[:, k, 0:1, :], ALU.subtract).then_inc(rest_made, 1)
            mark_sums()
            mark_far()
            all_groups(dve, group)
            last = (0, GROUPS - 1)
            residual(*last, 3)
            residual(*last, "edge", lambda: same_as_next(*last))
            variance(*last, lambda: scatter_index(*last))
            scales(*last)
            normalise(*last, range(ACT_NORM, BLOCKS), last=True)

        @block.gpsimd
        def _(pool):
            def gather(i, r):
                g, q = RING * i + r, r % RING
                pool.wait_ge(src_i_in[q], 16 * use(i, r))
                wait_alone(pool, turned, N_TURNS * (g - RING) + TURNS["src"] + 1)
                for j in range(QUAD):
                    pool.indirect_dma_start(src_x[:, q, j, :], None, x[:, :],
                                            bass.IndirectOffsetOnAxis(ap=src_i[:, q, j:j + 1], axis=0),
                                            bounds_check=N - 1, oob_is_err=False).then_inc(src_gathered[q], 16)
                pool.wait_ge(dst_i_in[q], 16 * use(i, r))
                wait_alone(pool, z_done, N_OUTS * (g - RING) + OUTS["edge"] + 1)
                for j in range(QUAD):
                    pool.indirect_dma_start(dst_x[:, q, j, :], None, x[:, :],
                                            bass.IndirectOffsetOnAxis(ap=dst_i[:, q, j:j + 1], axis=0),
                                            bounds_check=N - 1, oob_is_err=False).then_inc(dst_gathered[q], 16)

            def scatter(q, rows, index, done):
                for j in range(QUAD):
                    pool.indirect_dma_start(out[:, :], bass.IndirectOffsetOnAxis(ap=index[:, j:j + 1], axis=0),
                                            rows[:, j, :], None,
                                            bounds_check=N - 1, oob_is_err=False).then_inc(done, 16)

            def edge_rows_made(g):
                wait_alone(pool, act_normed, g + 1)
                wait_alone(pool, dve_normed, g + 1)
                wait_alone(pool, out_i_done, g + 1)

            def nodes_stored(i, r):
                q = r % RING
                wait_alone(pool, z_stored[q], 16 * use(i, r) + 16 * (q == 0))

            def near(g):
                return pool.value_load(far[:, bass.ds(g, 1)]) < 1

            def scatter_if_stored(i, r):
                g, q = RING * i + r, r % RING
                edge_rows_made(g)
                nodes_stored(i, r + 1)
                with pool.If(near(g)):
                    scatter(q, edge_z[:, q], out_i[:, q], scattered[q])
                with pool.Else():
                    rows = kept_rows[bass.ds(P * g, P), :].rearrange("p (j f) -> p j f", j=QUAD)
                    pool.dma_start(rows, edge_z[:, q]).then_inc(scattered[q], 16 * (QUAD - 1))
                    pool.dma_start(kept_index[bass.ds(P * g, P), :], out_i[:, q]).then_inc(scattered[q], 16)

            def group(i, r):
                gather(i, r)
                scatter_if_stored(i, r - PEEL)

            def place_edges():
                pool.iota(number_i[:, :], [[1, COLS]], base=0, channel_multiplier=COLS).then_inc(checks_made, 1)
                pool.iota(part_number_i[:, :], [[1, PART]], base=0, channel_multiplier=0).then_inc(checks_made, 1)
                with pool.Fori(0, E_PAD // PART) as part:
                    row = dst_pad[bass.ds(PART * part + 1, PART)].rearrange("(a w) -> a w", a=1).partition_broadcast(P)
                    pool.dma_start(part_i[:, :], row).then_inc(part_in, 16)
                    wait_alone(pool, part_ready, part + 1)
                pool.dma_start(pair_in[:, 0, :], whole(src_pad)).then_inc(pair_loaded, 16)
                pool.dma_start(pair_in[:, 1, :], whole(dst_pad[1:E_PAD + 1])).then_inc(pair_loaded, 16)
                pool.wait_ge(pair_loaded, 32)
                pool.wait_ge(placed, 1)
                with pool.Fori(0, COLS) as c:
                    pool.tensor_copy(pair_col[:, :], pair_in[:, :, bass.ds(c, 1)].rearrange("p k a -> p (k a)")).then_inc(col_made, 1)
                    pool.tensor_copy(place_col[:, :], places_i[:, bass.ds(c, 1)]).then_inc(col_made, 1)
                    wait_alone(pool, col_made, 2 * c + 2)
                    pool.indirect_dma_start(pairs[:, :], bass.IndirectOffsetOnAxis(ap=place_col[:, :], axis=0),
                                            pair_col[:, :], None, bounds_check=E_PAD - 1, oob_is_err=False).then_inc(rewritten, 16)
                    wait_alone(pool, rewritten, 16 * c + 16)
                done = 16 * COLS
                pool.dma_start(pair_tile[:, :, :], pairs.rearrange("(p c) k -> p c k", p=P)).then_inc(rewritten, 16)
                pool.wait_ge(rewritten, done + 16)
                pool.tensor_copy(pair_in[:, 0, :], pair_tile[:, :, 0]).then_inc(apart, 1)
                pool.tensor_copy(pair_in[:, 1, :], pair_tile[:, :, 1]).then_inc(apart, 1)
                pool.wait_ge(apart, 2)
                pool.dma_start(whole(src_pad), pair_in[:, 0, :]).then_inc(rewritten, 16)
                pool.dma_start(whole(dst_pad[1:E_PAD + 1]), pair_in[:, 1, :]).then_inc(rewritten, 16)
                pool.wait_ge(rewritten, done + 48)
                pool.dma_start(all_dst[:, :], whole(dst_pad[1:E_PAD + 1])).then_inc(rewritten, 16)
                pool.wait_ge(rewritten, done + 64)

            pool.memset(zeros_i[:, :], 0).then_inc(pads_made, 1)
            pool.memset(ends_i[:, 0:P], -1).then_inc(pads_made, 1)
            pool.memset(ends_i[:, P:], N).then_inc(pads_made, 1)
            pool.memset(ident[:, :], 0.0).then_inc(ident_made, 1)
            pool.wait_ge(ident_made, 1)
            pool.affine_select(ident[:, :], ident[:, :], [[-1, P]], ALU.not_equal, 1.0, base=0,
                               channel_multiplier=1).then_inc(ident_made, 1)
            pool.iota(checked_to[:, :], [[NODES, GROUPS]], base=FIRST_CHECK, channel_multiplier=0).then_inc(checks_made, 1)
            pool.wait_ge(unsorted_made, 1)
            with pool.If(pool.value_load(unsorted[:, :]) > 0):
                place_edges()
                pool.sem_inc(in_order, 1)
            with pool.Else():
                pool.sem_inc(in_order, 1)
            for r in range(PEEL):
                gather(0, r)
            pool.wait_ge(any_far_made, 1)
            with pool.Fori(0, LOOPS) as i:
                for r in range(PEEL, PEEL + RING):
                    group(i, r)
            for g in range(GROUPS - PEEL, CHECKED):
                scatter_if_stored(0, g)
            nodes_stored(0, GROUPS - 1)
            for g in range(CHECKED, GROUPS):
                edge_rows_made(g)
                scatter(g % RING, edge_z[:, g % RING], out_i[:, g % RING], scattered[g % RING])
            for q in range(RING):
                pool.wait_ge(scattered[q], 16 * QUAD * sum(1 for g in range(GROUPS) if g % RING == q))
            pool.wait_ge(any_far_made, 1)
            with pool.If(pool.value_load(any_far[:, :]) > 0):
                with pool.Fori(0, CHECKED) as g:
                    with pool.If(near(g)):
                        idle = src_pad[0:EDGES].rearrange("(p j) -> p j", j=QUAD)
                        pool.dma_start(back_i[:, :], idle).then_inc(back_in, 32)
                        wait_alone(pool, back_in, 32 * g + 32)
                        pool.dma_start(back_i[:, :], idle).then_inc(back_out, 16 * QUAD)
                    with pool.Else():
                        rows = kept_rows[bass.ds(P * g, P), :].rearrange("p (j f) -> p j f", j=QUAD)
                        pool.dma_start(back_rows[:, :, :], rows).then_inc(back_in, 16)
                        pool.dma_start(back_i[:, :], kept_index[bass.ds(P * g, P), :]).then_inc(back_in, 16)
                        wait_alone(pool, back_in, 32 * g + 32)
                        scatter(0, back_rows, back_i, back_out)
                    wait_alone(pool, back_out, 16 * QUAD * g + 16 * QUAD)
            with pool.Else():
                pool.sem_inc(waits_passed, 1)


_INS = ["x", "src", "dst", "L0_gnn_msg_w1", "L0_gnn_msg_b1", "L0_gnn_msg_w2", "L0_gnn_msg_b2",
        "L0_gnn_upd_w1", "L0_gnn_upd_b1", "L0_gnn_upd_w2", "L0_gnn_upd_b2"]


def kernel(**inputs):
    import concourse.bacc as bacc
    from concourse.bass_utils import run_bass_kernel_spmd

    nc = bacc.Bacc("TRN2", target_bir_lowering=False, num_devices=1)
    arrays, args = {}, []
    for name in _INS:
        a = np.ascontiguousarray(inputs[name])
        arrays[f"in_{name}"] = a
        args.append(nc.dram_tensor(f"in_{name}", a.shape, mybir.dt.from_np(a.dtype), kind="ExternalInput").ap())
    shape = inputs["x"].shape
    args.append(nc.dram_tensor("out_0", shape, F32, kind="ExternalOutput").ap())
    gnn_resnorm(nc, *args)
    r = run_bass_kernel_spmd(nc, [arrays], core_ids=[0])
    return r.results[0]["out_0"]
```

```python
from contextlib import ExitStack

import numpy as np
import concourse.bass as bass
from concourse import mybir

ALU = mybir.AluOpType
ACT = mybir.ActivationFunctionType
F32 = mybir.dt.float32
F32R = mybir.dt.float32r
BF16 = mybir.dt.bfloat16
I32 = mybir.dt.int32

P = 128
QUAD = 4
W = QUAD * P
ROWS = 16
NODES = P * ROWS
EDGES = W
NQ = ROWS // QUAD
RING = 4
PEEL = 5
EPS = 1e-5

TURNS = {0: 0, 1: 1, 2: 2, "src": 3, "dst": 4, 3: 5}
N_TURNS = len(TURNS)
LOWS = {0: 0, 1: 1, 2: 2, "src": 3, "dst": 4, 3: 5}
N_LOWS = len(LOWS)
OUTS = {0: 0, 1: 1, 2: 2, 3: 3, "edge": 4}
N_OUTS = len(OUTS)
BLOCKS = ROWS + QUAD
ACT_RUNS = [range(0, 4), range(4, 6), range(6, 11), range(11, 15)]
ACT_NORM = ACT_RUNS[-1].stop
DVE_RUNS = [range(15, 18), range(18, 20)]
ACT_END, DVE_END = [range(6, 8), range(8, 10)], [range(10, 12), range(12, 15)]
ACT_HALVES, DVE_HALVES = [range(0, 4), range(8, 12)], [range(4, 8), range(12, 16)]


def gnn_resnorm(nc, x, src, dst, msg_w1, msg_b1, msg_w2, msg_b2, upd_w1, upd_b1, upd_w2, upd_b2, out):
    N, D = x.shape
    E = src.shape[0]
    GROUPS = -(-N // NODES)
    SHORT = GROUPS * NODES - N
    E_PAD = GROUPS * EDGES
    assert D == P and E_PAD >= E and (GROUPS - PEEL) % RING == 0 and SHORT % ROWS == 0
    LOOPS = (GROUPS - PEEL) // RING
    COLS = E_PAD // P
    CHECKS = max(d for d in range(1, P + 1) if (E - 1) % d == 0)
    PART = E_PAD // 16
    FIRST_CHECK = 2 * NODES - SHORT
    FAR = 1 << 20
    CHECKED = GROUPS - 2
    SPLIT = 10
    assert E % SPLIT == 0 and N < FAR

    src_pad = nc.dram_tensor("src_pad", [E_PAD], I32).ap()
    dst_pad = nc.dram_tensor("dst_pad", [E_PAD + 2], I32).ap()
    goes_on = nc.dram_tensor("goes_on", [E_PAD], BF16).ap()
    pairs = nc.dram_tensor("pairs", [E_PAD, 2], I32).ap()
    kept_rows = nc.dram_tensor("kept_rows", [GROUPS * P, QUAD * P], F32).ap()
    kept_index = nc.dram_tensor("kept_index", [GROUPS * P, QUAD], I32).ap()

    with ExitStack() as ctx:
        def sb(name, shape, dt=F32):
            return ctx.enter_context(nc.sbuf_tensor(name, shape, dt))

        def sem(name):
            return ctx.enter_context(nc.semaphore(name))

        def sems(name):
            return [sem(f"{name}{q}") for q in range(RING)]

        turned_ps = ctx.enter_context(nc.psum_tensor("turned_ps", [P, 2, W], F32))
        pre_ps = ctx.enter_context(nc.psum_tensor("pre_ps", [P, 2, W], F32))
        out_ps = ctx.enter_context(nc.psum_tensor("out_ps", [P, 2, W], F32))
        edge_ps = ctx.enter_context(nc.psum_tensor("edge_ps", [P, 2, W], F32))

        w_msg1, w_upd1 = sb("w_msg1", [P, 2, P]), sb("w_upd1", [P, 2, P])
        w_m = w_upd1[:, 1, :]
        HIGH, LOW = 0, 1
        msg1_parts, upd1_parts = (sb(n, [P, 2, 2, P], F32R) for n in ("msg1_parts", "upd1_parts"))
        src_parts, dst_parts, x_parts = (
            [t[:, part, half, :] for part in (HIGH, LOW)]
            for t, half in ((msg1_parts, 0), (msg1_parts, 1), (upd1_parts, 0)))
        w_msg2, w_msg2T, w_fold, w_out, ident = (
            sb(n, [P, P]) for n in ("w_msg2", "w_msg2T", "w_fold", "w_out", "ident"))
        b_h, b_msg2, b_fold, b_u, eps = (sb(n, [P, 1]) for n in ("b_h", "b_msg2", "b_fold", "b_u", "eps"))
        b_row = sb("b_row", [1, 3, P])
        b_split = sb("b_split", [1, 3, QUAD, P], BF16)
        b_parts = sb("b_parts", [3, W], BF16)
        ones = sb("ones", [3, P], BF16)
        zeros_i = sb("zeros_i", [1, P], I32)
        ends_i = sb("ends_i", [1, 2 * P], I32)

        node_x = sb("node_x", [P, RING, ROWS, P])
        node_z = sb("node_z", [P, RING, ROWS, P])
        src_i = sb("src_i", [P, RING, QUAD], I32)
        dst_i = sb("dst_i", [P, RING, QUAD + 1], I32)
        same = sb("same", [P, RING, W], BF16)
        src_x = sb("src_x", [P, RING, QUAD, P])
        dst_x = sb("dst_x", [P, RING, QUAD, P])
        edge_z = sb("edge_z", [P, RING, QUAD, P])
        out_i = sb("out_i", [P, RING, QUAD], I32)
        same_i = sb("same_i", [P, QUAD], I32)

        node_xT = sb("node_xT", [P, 2, 2, W], F32R)
        node_u = sb("node_u", [P, 2, W])
        src_xT = sb("src_xT", [P, 2, W], F32R)
        dst_xT = sb("dst_xT", [P, 2, W], F32R)
        edge_h = sb("edge_h", [P, W])
        edge_m = sb("edge_m", [P, W])
        summed = sb("summed", [P, 2, W])
        edge_pre = sb("edge_pre", [P, W])
        edge_u = sb("edge_u", [P, W])

        stats = sb("stats", [P, 2, BLOCKS, 3])
        std = sb("std", [P, BLOCKS])
        scale, shift = sb("scale", [P, 2, BLOCKS]), sb("shift", [P, 2, BLOCKS])

        all_dst, all_before = (sb(n, [P, COLS], I32) for n in ("all_dst", "all_before"))
        this_dst, next_dst = (sb(n, [CHECKS, (E - 1) // CHECKS], I32) for n in ("this_dst", "next_dst"))
        all_same = sb("all_same", [P, COLS], BF16)
        ones_p = sb("ones_p", [P, 1])
        falls, falls_p = sb("falls", [CHECKS, (E - 1) // CHECKS]), sb("falls_p", [CHECKS, 1])
        unsorted = sb("unsorted", [1, 1], I32)
        last_dst, checked_to, far = (sb(n, [1, GROUPS], I32) for n in ("last_dst", "checked_to", "far"))
        any_far = sb("any_far", [1, 1], I32)
        pair_in, pair_tile = sb("pair_in", [P, 2, COLS], I32), sb("pair_tile", [P, COLS, 2], I32)
        pair_col, place_col = sb("pair_col", [P, 2], I32), sb("place_col", [P, 1], I32)
        dst_f, number, places, less, equal_before = (
            sb(n, [P, COLS]) for n in ("dst_f", "number", "places", "less", "equal_before"))
        number_i, places_i = sb("number_i", [P, COLS], I32), sb("places_i", [P, COLS], I32)
        part_i, part_f = sb("part_i", [P, PART], I32), sb("part_f", [P, PART])
        part_number_i, part_number = sb("part_number_i", [P, PART], I32), sb("part_number", [P, PART])
        part_hits, part_before = sb("part_hits", [P, PART], BF16), sb("part_before", [P, PART], BF16)

        back_rows = sb("back_rows", [P, QUAD, P])
        back_i = sb("back_i", [P, QUAD], I32)

        upd1_in, b_u_in, b_row_in, w_out_in, fold_in, message_weights_in, before_in = (
            sem(n) for n in ("upd1_in", "b_u_in", "b_row_in", "w_out_in", "fold_in", "message_weights_in", "before_in"))
        checks_in = sem("checks_in")
        waits_passed = sem("waits_passed")
        ident_made, pads_made, edges_ready = (sem(n) for n in ("ident_made", "pads_made", "edges_ready"))
        consts_made, split_made, rest_made, parts_in = (
            sem(n) for n in ("consts_made", "split_made", "rest_made", "parts_in"))
        set_pe, set_act = sem("set_pe"), sem("set_act")
        x_in, z_stored = sems("x_in"), sems("z_stored")
        src_i_in, dst_i_in, same_in = sems("src_i_in"), sems("dst_i_in"), sems("same_in")
        all_in, falls_made, falls_max, falls_added, unsorted_made = (
            sem(n) for n in ("all_in", "falls_made", "falls_max", "falls_added", "unsorted_made"))
        numbers_made, part_in, part_ready, compared, counted, places_made, placed = (
            sem(n) for n in ("numbers_made", "part_in", "part_ready", "compared", "counted", "places_made", "placed"))
        dst_f_made, number_moved, pair_loaded, col_made, apart, rewritten = (
            sem(n) for n in ("dst_f_made", "number_moved", "pair_loaded", "col_made", "apart", "rewritten"))
        in_order, all_same_made, goes_on_out = (sem(n) for n in ("in_order", "all_same_made", "goes_on_out"))
        checks_made, last_dst_in, far_made, any_far_made = (
            sem(n) for n in ("checks_made", "last_dst_in", "far_made", "any_far_made"))
        src_gathered, dst_gathered, scattered = sems("src_gathered"), sems("dst_gathered"), sems("scattered")
        turned, turn_copied = sem("turned"), sem("turn_copied")
        low_made, weights_high, weights_low = sem("low_made"), sem("weights_high"), sem("weights_low")
        pre_done, u_done = sem("pre_done"), sem("u_done")
        out_done, z_done, stats_done = sem("out_done"), sem("z_done"), sem("stats_done")
        h_pre, h_done, m_pre, m_done = (sem(n) for n in ("h_pre", "h_done", "m_pre", "m_done"))
        sum_done, edge_pre_ps, edge_pre_done, edge_u_done = (
            sem(n) for n in ("sum_done", "edge_pre_ps", "edge_pre_done", "edge_u_done"))
        same_i_done, out_i_done = sem("same_i_done"), sem("out_i_done")
        std_done, scale_done, shift_done = (sem(n) for n in ("std_done", "scale_done", "shift_done"))
        act_normed, dve_normed = sem("act_normed"), sem("dve_normed")
        helped, act_half, dve_half = sem("helped"), sem("act_half"), sem("dve_half")
        back_in, back_out = sem("back_in"), sem("back_out")

        def first_node(g):
            return 0 if isinstance(g, int) and g == 0 else NODES * g - SHORT

        def use(i, r):
            return i + r // RING + 1

        def wait(eng, s, value):
            if not isinstance(value, int) or value > 0:
                eng.wait_ge(s, value)

        def wait_alone(eng, s, value):
            wait(eng, s, value)
            if not isinstance(value, int):
                eng.sem_inc(waits_passed, 1)

        def all_groups(eng, group):
            for r in range(PEEL):
                group(0, r)
            with eng.Fori(0, LOOPS) as i:
                for r in range(PEEL, PEEL + RING):
                    group(i, r)

        def block_of(q, b):
            return node_z[:, q, b, :] if b < ROWS else edge_z[:, q, b - ROWS, :]

        def whole(a):
            return a.rearrange("(p c) -> p c", p=P)

        def stores_of(q):
            return 16 * sum(1 + (g in (0, GROUPS - 1)) for g in range(GROUPS) if g % RING == q)

        block = ctx.enter_context(nc.Block())

        @block.sync
        def _(sp):
            def load_x(i, r):
                g, q = RING * i + r, r % RING
                wait(sp, z_done, N_OUTS * (g - RING) + OUTS[3] + 1)
                rows = x[bass.ds(first_node(g), NODES), :].rearrange("(p j) f -> p j f", j=ROWS)
                sp.dma_start(node_x[:, q], rows).then_inc(x_in[q], 16)

            def load_edges(i, r):
                load_ends(i, r)
                load_same(i, r)

            def load_ends(i, r):
                g, q = RING * i + r, r % RING
                if not isinstance(g, int) or g >= RING:
                    wait_alone(sp, src_gathered[q], 16 * QUAD * (use(i, r) - 1))
                    wait_alone(sp, dst_gathered[q], 16 * QUAD * (use(i, r) - 1))
                    sp.wait_ge(out_i_done, g - RING + 1)
                s = src_pad[bass.ds(EDGES * g, EDGES)].rearrange("(p j) -> p j", j=QUAD)
                sp.dma_start(src_i[:, q, :], s).then_inc(src_i_in[q], 16)
                d = dst_pad[bass.ds(EDGES * g + 1, EDGES)]
                d = bass.AP(d.tensor, d.offset, [[QUAD, P], [1, QUAD + 1]])
                sp.dma_start(dst_i[:, q, :], d).then_inc(dst_i_in[q], 16)

            def load_same(i, r):
                g, q = RING * i + r, r % RING
                wait_alone(sp, sum_done, g - RING + 1)
                row = goes_on[bass.ds(EDGES * g, EDGES)].rearrange("(a w) -> a w", a=1).partition_broadcast(P)
                sp.dma_start(same[:, q, :], row).then_inc(same_in[q], 16)

            def store(i, r):
                g, q = RING * i + r, r % RING
                sp.wait_ge(act_normed, g + 1)
                sp.wait_ge(dve_normed, g + 1)
                if isinstance(g, int) and g == 0:
                    full = (NODES - SHORT) // ROWS
                    for a, b in ((0, full // 8 * 8), (full // 8 * 8, full)):
                        rows = out[a * ROWS:b * ROWS, :].rearrange("(p j) f -> p j f", j=ROWS)
                        sp.dma_start(rows, node_z[a:b, q]).then_inc(z_stored[q], 16)
                    return
                rows = out[bass.ds(first_node(g), NODES), :].rearrange("(p j) f -> p j f", j=ROWS)
                sp.dma_start(rows, node_z[:, q]).then_inc(z_stored[q], 16)

            def lists(name):
                return name.rearrange("(a b) -> a b", a=SPLIT)

            for tile, first in ((this_dst, 0), (next_dst, 1)):
                sp.dma_start(tile[:, :], dst[first:first + E - 1].rearrange("(p c) -> p c", p=CHECKS)).then_inc(checks_in, 16)
            sp.dma_start(lists(dst_pad[1:E + 1]), lists(dst)).then_inc(edges_ready, 16)
            sp.dma_start(lists(src_pad[0:E]), lists(src)).then_inc(edges_ready, 16)
            halves = "(k p) f -> p k f"
            sp.dma_start(w_upd1[:, :, :], upd_w1.rearrange(halves, p=P)).then_inc(upd1_in, 16)
            sp.wait_ge(pads_made, 3)
            n_pad = E_PAD - E
            sp.dma_start(dst_pad[0:1].rearrange("(a b) -> a b", a=1), ends_i[:, 0:1]).then_inc(edges_ready, 16)
            sp.dma_start(dst_pad[E + 1:].rearrange("(a b) -> a b", a=1), ends_i[:, P:P + n_pad + 1]).then_inc(edges_ready, 16)
            sp.dma_start(src_pad[E:E_PAD].rearrange("(a b) -> a b", a=1), zeros_i[:, 0:n_pad]).then_inc(edges_ready, 16)
            sp.dma_start(b_row[:, 0, :], upd_b2.rearrange("(a f) -> a f", a=1)).then_inc(b_row_in, 16)
            sp.wait_ge(edges_ready, 16 * 5)
            sp.dma_start(all_dst[:, :], whole(dst_pad[1:1 + E_PAD])).then_inc(all_in, 16)
            sp.wait_ge(in_order, 1)
            load_ends(0, 0)
            load_x(0, 0)

            def load_bias(tile, array, loaded):
                with nc.allow_non_contiguous_dma(reason="one bias in a partition"):
                    sp.dma_start(tile[:, :], array.rearrange("(p a) -> p a", a=1)).then_inc(loaded, 16)

            load_bias(b_u, upd_b1, b_u_in)
            sp.dma_start(w_out[:, :], upd_w2).then_inc(w_out_in, 16)
            sp.dma_start(w_msg2[:, :], msg_w2).then_inc(fold_in, 16)
            load_bias(b_msg2, msg_b2, fold_in)
            sp.dma_start(w_msg1[:, :, :], msg_w1.rearrange(halves, p=P)).then_inc(message_weights_in, 16)
            load_bias(b_h, msg_b1, message_weights_in)
            sp.dma_start(all_before[:, :], whole(dst_pad[0:E_PAD])).then_inc(before_in, 16)
            sp.wait_ge(split_made, 3)
            for k in range(3):
                sp.dma_start(b_parts[k:k + 1, :], b_split[:, k, :, :].rearrange("a q f -> a (q f)")).then_inc(parts_in, 16)
            load_ends(0, 1)
            load_x(0, 1)
            sp.wait_ge(all_same_made, 1)
            sp.dma_start(whole(goes_on), all_same[:, :]).then_inc(goes_on_out, 16)
            with nc.allow_non_contiguous_dma(reason="one destination a group"):
                sp.dma_start(last_dst[:, :], dst_pad[1:E_PAD + 1].rearrange("(a g w) -> a g w", a=1, w=EDGES)[:, :, EDGES - 1]).then_inc(last_dst_in, 16)
            sp.wait_ge(goes_on_out, 16)
            load_same(0, 0)
            load_same(0, 1)
            for r in range(2, PEEL):
                sp.wait_ge(dst_gathered[r - 2], 16 * QUAD)
                load_x(0, r)
                load_edges(0, r)
            store(0, 0)
            with sp.Fori(0, LOOPS) as i:
                for r in range(PEEL, PEEL + RING):
                    load_x(i, r)
                    load_edges(i, r)
                    store(i, r - RING)
            for g in range(GROUPS - RING, GROUPS - 2):
                store(0, g)
            sp.wait_ge(helped, 1)
            store(0, GROUPS - 2)
            g, q = GROUPS - 1, (GROUPS - 1) % RING
            rows = out[first_node(g):first_node(g) + NODES, :].rearrange("(p j) f -> p j f", j=ROWS)
            half = ROWS // 2
            sp.wait_ge(act_half, 1)
            sp.wait_ge(dve_half, 1)
            sp.dma_start(rows[:, 0:half], node_z[:, q, 0:half]).then_inc(z_stored[q], 16)
            sp.wait_ge(act_normed, GROUPS)
            sp.wait_ge(dve_half, 2)
            sp.dma_start(rows[:, half:], node_z[:, q, half:]).then_inc(z_stored[q], 16)
            for q in range(RING):
                sp.wait_ge(z_stored[q], stores_of(q))

        @block.tensor
        def _(pe):
            def turn(i, r, what):
                g, q = RING * i + r, r % RING
                order, bank = N_TURNS * g + TURNS[what], TURNS[what] % 2
                rows = {"src": src_x, "dst": dst_x}.get(what, node_x)
                first = 0 if what in ("src", "dst") else QUAD * what
                if what == "src":
                    pe.wait_ge(src_gathered[q], 16 * QUAD * use(i, r))
                elif what == "dst":
                    pe.wait_ge(dst_gathered[q], 16 * QUAD * use(i, r))
                elif what == 0:
                    pe.wait_ge(x_in[q], 16 * use(i, r))
                wait(pe, turn_copied, order - 1)
                before = next(w for w in TURNS if TURNS[w] == (TURNS[what] - 2) % N_TURNS)
                wait(pe, low_made, N_LOWS * (g - (TURNS[what] < 2)) + LOWS[before] + 1)
                for j in range(QUAD):
                    t = pe.transpose(turned_ps[:, bank, j * P:(j + 1) * P], rows[:, q, first + j, :], ident[:, :])
                t.then_inc(turned, 1)

            def product(to, weight, xT, start=True, stop=True, low_ready=lambda: None):
                pe.matmul(to, weight[LOW], xT[:, HIGH, :], start=start, stop=False)
                pe.matmul(to, weight[HIGH], xT[:, HIGH, :], start=False, stop=False)
                low_ready()
                return pe.matmul(to, weight[HIGH], xT[:, LOW, :], start=False, stop=stop)

            def node_pre(i, r, k):
                g = RING * i + r
                pe.wait_ge(turn_copied, N_TURNS * g + TURNS[k] + 1)
                if r == 0:
                    pe.wait_ge(weights_high, 1)
                    pe.wait_ge(weights_low, 1)
                wait(pe, u_done, NQ * g + k - 1)
                product(pre_ps[:, k % 2, :], x_parts, node_xT[:, k % 2],
                        low_ready=lambda: pe.wait_ge(low_made, N_LOWS * g + LOWS[k] + 1)).then_inc(pre_done, 1)

            def bias_out(i, r, what):
                g = RING * i + r
                order, bank = N_OUTS * g + OUTS[what], (r * N_OUTS + OUTS[what]) % 2
                wait(pe, z_done, order - 1)
                if r == 0 and what == 0:
                    pe.wait_ge(consts_made, 2)
                    pe.wait_ge(unsorted_made, 1)
                    pe.wait_ge(parts_in, 16 * 3)
                    pe.wait_ge(w_out_in, 16)
                pe.matmul(out_ps[:, bank, :], ones[:, :], b_parts[:, :], start=True, stop=False, skip_group_check=True)

            def rows_out(i, r, what, with_bias=True):
                g = RING * i + r
                bank = (r * N_OUTS + OUTS[what]) % 2
                if with_bias:
                    bias_out(i, r, what)
                if what == "edge":
                    pe.wait_ge(edge_u_done, g + 1)
                    u = edge_u
                else:
                    pe.wait_ge(u_done, NQ * g + what + 1)
                    u = node_u[:, what % 2, :]
                for j in range(QUAD):
                    y = pe.matmul(out_ps[:, bank, j * P:(j + 1) * P], u[:, j * P:(j + 1) * P], w_out[:, :],
                                  start=False, stop=(j == QUAD - 1), skip_group_check=True)
                y.then_inc(out_done, 1)

            def ends_pre(i, r):
                g = RING * i + r
                pe.wait_ge(turn_copied, N_TURNS * g + TURNS["dst"] + 1)
                if isinstance(g, int) and g == 0:
                    pe.wait_ge(weights_high, 2)
                    pe.wait_ge(weights_low, 2)
                    pe.wait_ge(set_act, 3)
                wait(pe, edge_pre_done, g)
                product(edge_ps[:, 0, :], src_parts, src_xT, stop=False,
                        low_ready=lambda: pe.wait_ge(low_made, N_LOWS * g + LOWS["src"] + 1))
                product(edge_ps[:, 0, :], dst_parts, dst_xT, start=False,
                        low_ready=lambda: pe.wait_ge(low_made, N_LOWS * g + LOWS["dst"] + 1)).then_inc(h_pre, 1)

            def message(i, r):
                g = RING * i + r
                pe.wait_ge(h_done, g + 1)
                wait(pe, m_done, g)
                pe.matmul(edge_ps[:, 1, :], w_fold[:, :], edge_h[:, :], start=True, stop=True).then_inc(m_pre, 1)

            def destination_pre(i, r):
                product(edge_ps[:, 0, :], x_parts, dst_xT).then_inc(edge_pre_ps, 1)

            def fold():
                pe.wait_ge(upd1_in, 16)
                pe.wait_ge(fold_in, 16 * 2)
                pe.transpose(edge_ps[:, 0, 0:P], w_msg2[:, :], ident[:, :]).then_inc(set_pe, 1)
                pe.wait_ge(set_act, 1)
                pe.matmul(edge_ps[:, 1, 0:P], w_msg2T[:, :], w_m, start=True, stop=True)
                pe.matmul(edge_ps[:, 1, P:P + 1], w_m, b_msg2[:, :], start=True, stop=True).then_inc(set_pe, 1)

            def group(i, r):
                before = (i, r - 1)
                turn(i, r, 0)
                if r:
                    rows_out(*before, 3)
                turn(i, r, 1)
                if r:
                    bias_out(*before, "edge")
                node_pre(i, r, 0)
                turn(i, r, 2)
                if r:
                    rows_out(*before, "edge", with_bias=False)
                node_pre(i, r, 1)
                rows_out(i, r, 0)
                if r == 0:
                    fold()
                turn(i, r, "src")
                turn(i, r, "dst")
                node_pre(i, r, 2)
                rows_out(i, r, 1)
                ends_pre(i, r)
                turn(i, r, 3)
                rows_out(i, r, 2)
                message(i, r)
                node_pre(i, r, 3)
                destination_pre(i, r)

            pe.wait_ge(falls_max, 1)
            pe.wait_ge(numbers_made, 1)
            pe.matmul(out_ps[0:1, 1, 0:1], falls_p[:, :], ones_p[0:CHECKS, :], start=True, stop=True).then_inc(falls_added, 1)
            pe.wait_ge(ident_made, 2)
            all_groups(pe, group)
            rows_out(0, GROUPS - 1, 3)
            rows_out(0, GROUPS - 1, "edge")

        @block.scalar
        def _(act):
            def copy_turned(i, r, what):
                g = RING * i + r
                order, bank = N_TURNS * g + TURNS[what], TURNS[what] % 2
                act.wait_ge(turned, order + 1)
                if what == "src":
                    wait(act, h_pre, g)
                    to = src_xT[:, HIGH, :]
                elif what == "dst":
                    wait(act, edge_pre_ps, g)
                    to = dst_xT[:, HIGH, :]
                else:
                    wait(act, pre_done, NQ * g + what - 1)
                    to = node_xT[:, what % 2, HIGH, :]
                act.activation(to, turned_ps[:, bank, :], ACT.Copy).then_inc(turn_copied, 1)

            def node_relu(i, r, k):
                g = RING * i + r
                act.wait_ge(pre_done, NQ * g + k + 1)
                wait(act, out_done, N_OUTS * g + OUTS[k - 2] + 1 if k >= 2 else N_OUTS * (g - 1) + OUTS[k + 2] + 1)
                act.activation(node_u[:, k % 2, :], pre_ps[:, k % 2, :], ACT.Relu, bias=b_u[:, :]).then_inc(u_done, 1)

            def edge_relu(i, r):
                g = RING * i + r
                act.wait_ge(edge_pre_done, g + 1)
                wait(act, out_done, N_OUTS * (g - 1) + OUTS["edge"] + 1)
                act.activation(edge_u[:, :], edge_pre[:, :], ACT.Relu, bias=b_u[:, :]).then_inc(edge_u_done, 1)

            def deviation(i, r, blocks=slice(0, BLOCKS), quads=N_OUTS):
                g = RING * i + r
                act.wait_ge(stats_done, N_OUTS * g + quads)
                wait(act, scale_done, g)
                act.activation(std[:, blocks], stats[:, r % 2, blocks, 2], ACT.Sqrt, bias=eps[:, :], scale=1.0 / P).then_inc(std_done, 1)

            def normalise(i, r, blocks, last=False):
                g, q = RING * i + r, r % RING
                act.wait_ge(shift_done, g + 1)
                for b in blocks:
                    z = block_of(q, b)
                    scaled = act.activation(z, z, ACT.Identity, bias=shift[:, r % 2, b:b + 1], scale=scale[:, r % 2, b:b + 1])
                if last:
                    scaled.then_inc(act_normed, 1)
                return scaled

            def ends_relu(i, r):
                g = RING * i + r
                act.wait_ge(h_pre, g + 1)
                wait(act, m_pre, g)
                act.activation(edge_h[:, :].rearrange("f (p j) -> f j p", j=QUAD),
                               edge_ps[:, 0, :].rearrange("f (j p) -> f j p", j=QUAD), ACT.Relu,
                               bias=b_h[:, :]).then_inc(h_done, 1)

            def message_bias(i, r):
                g = RING * i + r
                act.wait_ge(m_pre, g + 1)
                wait(act, sum_done, g)
                act.activation(edge_m[:, :], edge_ps[:, 1, :], ACT.Identity, bias=b_fold[:, :]).then_inc(m_done, 1)

            def fold():
                act.wait_ge(set_pe, 1)
                act.activation(w_msg2T[:, :], edge_ps[:, 0, 0:P], ACT.Copy).then_inc(set_act, 1)
                act.wait_ge(message_weights_in, 16 * 2)
                act.activation(msg1_parts[:, HIGH], w_msg1[:, :, :], ACT.Copy).then_inc(weights_high, 1)
                act.wait_ge(set_pe, 2)
                act.activation(w_fold[:, :], edge_ps[:, 1, 0:P], ACT.Copy).then_inc(set_act, 1)
                act.activation(b_fold[:, :], edge_ps[:, 1, P:P + 1], ACT.Copy).then_inc(set_act, 1)
                act.wait_ge(set_act, 3)
                act.wait_ge(consts_made, 2)

            def group(i, r):
                before, twice_before = (i, r - 1), (i, r - 2)
                copy_turned(i, r, 0)
                if r == 0:
                    act.wait_ge(b_u_in, 16)
                if r:
                    edge_relu(*before)
                copy_turned(i, r, 1)
                node_relu(i, r, 0)
                copy_turned(i, r, 2)
                if r > 1:
                    normalise(*twice_before, ACT_RUNS[2])
                node_relu(i, r, 1)
                if r == 0:
                    fold()
                if r:
                    deviation(*before)
                copy_turned(i, r, "src")
                copy_turned(i, r, "dst")
                node_relu(i, r, 2)
                if r > 1:
                    normalise(*twice_before, ACT_RUNS[3], last=True)
                ends_relu(i, r)
                copy_turned(i, r, 3)
                if r:
                    normalise(*before, ACT_RUNS[0])
                message_bias(i, r)
                node_relu(i, r, 3)
                if r:
                    normalise(*before, ACT_RUNS[1])

            act.wait_ge(upd1_in, 16)
            act.activation(upd1_parts[:, HIGH], w_upd1[:, :, :], ACT.Copy).then_inc(weights_high, 1)
            all_groups(act, group)
            last, before = (0, GROUPS - 1), (0, GROUPS - 2)
            normalise(*before, ACT_END[0])
            edge_relu(*last)
            normalise(*before, ACT_END[1], last=True)
            deviation(*last, slice(0, ROWS), quads=NQ)
            normalise(*last, ACT_HALVES[0]).then_inc(act_half, 1)
            deviation(*last, slice(ROWS, BLOCKS))
            normalise(*last, ACT_HALVES[1], last=True)

        @block.vector
        def _(dve):
            def low_part(i, r, what):
                g = RING * i + r
                bank = TURNS[what] % 2
                to = {"src": src_xT, "dst": dst_xT}[what] if what in ("src", "dst") else node_xT[:, what % 2]
                dve.wait_ge(turn_copied, N_TURNS * g + TURNS[what] + 1)
                dve.tensor_tensor(to[:, LOW, :], turned_ps[:, bank, :], to[:, HIGH, :], ALU.subtract).then_inc(low_made, 1)

            def residual(i, r, what, between=lambda: None):
                g, q = RING * i + r, r % RING
                order, bank = N_OUTS * g + OUTS[what], (r * N_OUTS + OUTS[what]) % 2
                if what == "edge":
                    if not isinstance(g, int) or g >= RING:
                        dve.wait_ge(scattered[q], 16 * QUAD * (use(i, r) - 1))
                    z, rows, b0 = edge_z[:, q], dst_x[:, q], ROWS
                else:
                    if what == 0 and (not isinstance(g, int) or g >= RING):
                        dve.wait_ge(z_stored[q], 16 * (use(i, r) - 1) + 16 * (q == 0))
                    b0 = QUAD * what
                    z, rows = node_z[:, q, b0:b0 + QUAD, :], node_x[:, q, b0:b0 + QUAD, :]
                dve.wait_ge(out_done, order + 1)
                dve.tensor_tensor(z, out_ps[:, bank, :].rearrange("p (j f) -> p j f", j=QUAD), rows, ALU.add).then_inc(z_done, 1)
                between()
                dve.wait_ge(z_done, order + 1)
                for j in range(0, QUAD, 2):
                    s = dve.bn_stats(stats[:, r % 2, b0 + j:b0 + j + 2, :].rearrange("p b s -> p (b s)"),
                                     z[:, j:j + 2, :].rearrange("p b f -> p f b"))
                s.then_inc(stats_done, 1)

            def inverse_deviation(i, r, blocks=slice(0, BLOCKS), n=1):
                g = RING * i + r
                dve.wait_ge(std_done, g + n)
                wait(dve, act_normed, g - 1)
                dve.reciprocal(scale[:, r % 2, blocks], std[:, blocks]).then_inc(scale_done, 1)

            def shifts(i, r, blocks=slice(0, BLOCKS), n=1):
                g = RING * i + r
                dve.wait_ge(scale_done, g + n)
                dve.scalar_tensor_tensor(shift[:, r % 2, blocks], stats[:, r % 2, blocks, 1], -1.0, scale[:, r % 2, blocks], ALU.mult, ALU.mult).then_inc(shift_done, 1)

            def normalise(i, r, blocks, last=False, n=1):
                g, q = RING * i + r, r % RING
                dve.wait_ge(shift_done, g + n)
                for b in blocks:
                    z = block_of(q, b)
                    scaled = dve.tensor_scalar(z, z, scale[:, r % 2, b:b + 1], shift[:, r % 2, b:b + 1], ALU.mult, ALU.add)
                if last:
                    scaled.then_inc(dve_normed, 1)
                return scaled

            def same_as_next(i, r):
                g, q = RING * i + r, r % RING
                dve.wait_ge(dst_i_in[q], 16 * use(i, r))
                dve.tensor_tensor(same_i[:, :], dst_i[:, q, 0:QUAD], dst_i[:, q, 1:], ALU.is_equal).then_inc(same_i_done, 1)

            def scatter_index(i, r):
                g, q = RING * i + r, r % RING
                dve.wait_ge(same_i_done, g + 1)
                dve.scalar_tensor_tensor(out_i[:, q, :], same_i[:, :], float(FAR), dst_i[:, q, 0:QUAD],
                                         ALU.mult, ALU.add).then_inc(out_i_done, 1)

            def sum_edges(i, r):
                g = RING * i + r
                dve.wait_ge(m_done, g + 1)
                dve.wait_ge(same_in[r % RING], 16 * use(i, r))
                first = isinstance(g, int) and g == 0
                wait(dve, sum_done, g)
                dve.tensor_tensor_scan(summed[:, r % 2, :], same[:, r % RING, :], edge_m[:, :],
                                       0.0 if first else summed[:, (r - 1) % 2, W - 1:W],
                                       ALU.mult, ALU.add).then_inc(sum_done, 1)

            def edge_update(i, r):
                g = RING * i + r
                dve.wait_ge(edge_pre_ps, g + 1)
                dve.wait_ge(sum_done, g + 1)
                wait(dve, edge_u_done, g)
                dve.tensor_tensor(edge_pre[:, :].rearrange("f (j p) -> f j p", j=QUAD),
                                  edge_ps[:, 0, :].rearrange("f (j p) -> f j p", j=QUAD),
                                  summed[:, r % 2, :].rearrange("f (p j) -> f j p", j=QUAD),
                                  ALU.add).then_inc(edge_pre_done, 1)

            def group(i, r):
                before = (i, r - 1)
                low_part(i, r, 0)
                if r:
                    residual(*before, 3, lambda: low_part(i, r, 1))
                    residual(*before, "edge", lambda: low_part(i, r, 2))
                else:
                    low_part(i, r, 1)
                    low_part(i, r, 2)
                    mark_sums()
                residual(i, r, 0, lambda: same_as_next(*before) if r else None)
                if r == 0:
                    weights_low_part(1, msg1_parts, w_msg1, message_weights_in, 16 * 2)
                low_part(i, r, "src")
                if r:
                    inverse_deviation(*before)
                    scatter_index(*before)
                    shifts(*before)
                low_part(i, r, "dst")
                residual(i, r, 1, lambda: normalise(*before, DVE_RUNS[0]) if r else None)
                low_part(i, r, 3)
                residual(i, r, 2, lambda: normalise(*before, DVE_RUNS[1], last=True) if r else None)
                sum_edges(i, r)
                edge_update(i, r)
                if r == 0:
                    mark_far()

            def order_edges():
                dve.memset(ones_p[:, :], 1.0).then_inc(numbers_made, 1)
                dve.wait_ge(checks_in, 16 * 2)
                dve.tensor_tensor(falls[:, :], this_dst[:, :], next_dst[:, :], ALU.is_gt).then_inc(falls_made, 1)
                dve.wait_ge(falls_made, 1)
                dve.tensor_reduce(falls_p[:, :], falls[:, :], mybir.AxisListType.X, ALU.max).then_inc(falls_max, 1)
                dve.wait_ge(falls_added, 1)
                dve.tensor_copy(unsorted[:, :], out_ps[0:1, 1, 0:1]).then_inc(unsorted_made, 1)
                dve.wait_ge(unsorted_made, 1)
                with dve.If(dve.value_load(unsorted[:, :]) > 0):
                    count_places()
                with dve.Else():
                    dve.sem_inc(waits_passed, 1)

            def weights_low_part(n, parts, weights, loaded, count):
                dve.wait_ge(loaded, count)
                dve.wait_ge(weights_high, n + 1)
                dve.tensor_tensor(parts[:, LOW], weights[:, :, :], parts[:, HIGH], ALU.subtract).then_inc(weights_low, 1)

            def mark_sums():
                dve.wait_ge(in_order, 1)
                dve.wait_ge(all_in, 16)
                dve.wait_ge(before_in, 16)
                dve.tensor_tensor(all_same[:, :], all_dst[:, :], all_before[:, :], ALU.is_equal).then_inc(all_same_made, 1)

            def mark_far():
                dve.wait_ge(last_dst_in, 16)
                dve.wait_ge(checks_made, 1)
                dve.tensor_tensor(far[:, :], last_dst[:, :], checked_to[:, :], ALU.is_ge).then_inc(far_made, 1)
                dve.wait_ge(far_made, 1)
                dve.tensor_reduce(any_far[:, :], far[:, 0:CHECKED], mybir.AxisListType.X, ALU.max).then_inc(any_far_made, 1)

            def count_places():
                dve.wait_ge(checks_made, 3)
                dve.wait_ge(all_in, 16)
                dve.tensor_copy(dst_f[:, :], all_dst[:, :]).then_inc(dst_f_made, 1)
                dve.tensor_copy(number[:, :], number_i[:, :]).then_inc(dst_f_made, 1)
                dve.tensor_copy(part_number[:, :], part_number_i[:, :]).then_inc(dst_f_made, 1)
                dve.memset(places[:, :], 0.0).then_inc(dst_f_made, 1)
                dve.wait_ge(dst_f_made, 4)
                with dve.Fori(0, E_PAD // PART) as part:
                    dve.wait_ge(part_in, 16 * part + 16)
                    dve.tensor_copy(part_f[:, :], part_i[:, :]).then_inc(part_ready, 1)
                    wait_alone(dve, part_ready, part + 1)
                    with dve.Fori(0, COLS) as c:
                        edge, at = dst_f[:, bass.ds(c, 1)], number[:, bass.ds(c, 1)]
                        dve.tensor_scalar(part_hits[:, :], part_f[:, :], edge, None, ALU.is_lt, ALU.add,
                                          accum_out=less[:, bass.ds(c, 1)]).then_inc(compared, 1)
                        dve.tensor_scalar(part_before[:, :], part_number[:, :], at, None, ALU.is_lt).then_inc(compared, 1)
                        dve.wait_ge(compared, part * (3 * COLS) + 3 * c + 2)
                        dve.scalar_tensor_tensor(part_hits[:, :], part_f[:, :], edge, part_before[:, :], ALU.is_equal,
                                                 ALU.mult, accum_out=equal_before[:, bass.ds(c, 1)]).then_inc(compared, 1)
                        dve.wait_ge(compared, part * (3 * COLS) + 3 * c + 3)
                    dve.tensor_tensor(places[:, :], places[:, :], less[:, :], ALU.add).then_inc(counted, 1)
                    dve.wait_ge(counted, part * 3 + 1)
                    dve.tensor_tensor(places[:, :], places[:, :], equal_before[:, :], ALU.add).then_inc(counted, 1)
                    dve.tensor_scalar(number[:, :], number[:, :], float(-PART), None, ALU.add).then_inc(counted, 1)
                    dve.wait_ge(counted, part * 3 + 3)
                dve.tensor_copy(places_i[:, :], places[:, :]).then_inc(placed, 1)

            dve.memset(ones[:, :], 1.0).then_inc(consts_made, 1)
            dve.memset(eps[:, :], EPS).then_inc(consts_made, 1)
            order_edges()
            dve.wait_ge(b_row_in, 16)
            for k in range(3):
                part = b_row[:, k:k + 1, :]
                if k:
                    dve.wait_ge(rest_made, k)
                for j in range(QUAD):
                    c = dve.tensor_copy(b_split[:, k, j:j + 1, :], part)
                c.then_inc(split_made, 1)
                if k < 2:
                    dve.wait_ge(split_made, k + 1)
                    dve.tensor_tensor(b_row[:, k + 1:k + 2, :], part, b_split[:, k, 0:1, :], ALU.subtract).then_inc(rest_made, 1)
            weights_low_part(0, upd1_parts, w_upd1, upd1_in, 16)
            all_groups(dve, group)
            last = (0, GROUPS - 1)
            before = (0, GROUPS - 2)
            residual(*last, 3, lambda: normalise(*before, DVE_END[0]))
            normalise(*before, DVE_END[1]).then_inc(helped, 1)
            inverse_deviation(*last, slice(0, ROWS))
            same_as_next(*last)
            shifts(*last, slice(0, ROWS))
            residual(*last, "edge", lambda: scatter_index(*last))
            normalise(*last, DVE_HALVES[0]).then_inc(dve_half, 1)
            normalise(*last, DVE_HALVES[1]).then_inc(dve_half, 1)
            inverse_deviation(*last, slice(ROWS, BLOCKS), n=2)
            shifts(*last, slice(ROWS, BLOCKS), n=2)
            normalise(*last, range(ROWS, BLOCKS), last=True, n=2)

        @block.gpsimd
        def _(pool):
            def gather(i, r):
                g, q = RING * i + r, r % RING
                pool.wait_ge(src_i_in[q], 16 * use(i, r))
                wait_alone(pool, turned, N_TURNS * (g - RING) + TURNS["src"] + 1)
                for j in range(QUAD):
                    pool.indirect_dma_start(src_x[:, q, j, :], None, x[:, :],
                                            bass.IndirectOffsetOnAxis(ap=src_i[:, q, j:j + 1], axis=0),
                                            bounds_check=N - 1, oob_is_err=False).then_inc(src_gathered[q], 16)
                pool.wait_ge(dst_i_in[q], 16 * use(i, r))
                wait_alone(pool, z_done, N_OUTS * (g - RING) + OUTS["edge"] + 1)
                for j in range(QUAD):
                    pool.indirect_dma_start(dst_x[:, q, j, :], None, x[:, :],
                                            bass.IndirectOffsetOnAxis(ap=dst_i[:, q, j:j + 1], axis=0),
                                            bounds_check=N - 1, oob_is_err=False).then_inc(dst_gathered[q], 16)

            def scatter(q, rows, index, done):
                for j in range(QUAD):
                    pool.indirect_dma_start(out[:, :], bass.IndirectOffsetOnAxis(ap=index[:, j:j + 1], axis=0),
                                            rows[:, j, :], None,
                                            bounds_check=N - 1, oob_is_err=False).then_inc(done, 16)

            def edge_rows_made(g):
                wait_alone(pool, act_normed, g + 1)
                wait_alone(pool, dve_normed, g + 1)
                wait_alone(pool, out_i_done, g + 1)

            def nodes_stored(i, r):
                q = r % RING
                wait_alone(pool, z_stored[q], 16 * use(i, r) + 16 * (q == 0))

            def near(g):
                return pool.value_load(far[:, bass.ds(g, 1)]) < 1

            def scatter_if_stored(i, r):
                g, q = RING * i + r, r % RING
                edge_rows_made(g)
                nodes_stored(i, r + 1)
                with pool.If(near(g)):
                    scatter(q, edge_z[:, q], out_i[:, q], scattered[q])
                with pool.Else():
                    rows = kept_rows[bass.ds(P * g, P), :].rearrange("p (j f) -> p j f", j=QUAD)
                    pool.dma_start(rows, edge_z[:, q]).then_inc(scattered[q], 16 * (QUAD - 1))
                    pool.dma_start(kept_index[bass.ds(P * g, P), :], out_i[:, q]).then_inc(scattered[q], 16)

            def group(i, r):
                gather(i, r)
                scatter_if_stored(i, r - PEEL)

            def place_edges():
                pool.wait_ge(edges_ready, 16 * 5)
                pool.iota(number_i[:, :], [[1, COLS]], base=0, channel_multiplier=COLS).then_inc(checks_made, 1)
                pool.iota(part_number_i[:, :], [[1, PART]], base=0, channel_multiplier=0).then_inc(checks_made, 1)
                with pool.Fori(0, E_PAD // PART) as part:
                    row = dst_pad[bass.ds(PART * part + 1, PART)].rearrange("(a w) -> a w", a=1).partition_broadcast(P)
                    pool.dma_start(part_i[:, :], row).then_inc(part_in, 16)
                    wait_alone(pool, part_ready, part + 1)
                pool.dma_start(pair_in[:, 0, :], whole(src_pad)).then_inc(pair_loaded, 16)
                pool.dma_start(pair_in[:, 1, :], whole(dst_pad[1:E_PAD + 1])).then_inc(pair_loaded, 16)
                pool.wait_ge(pair_loaded, 32)
                pool.wait_ge(placed, 1)
                with pool.Fori(0, COLS) as c:
                    pool.tensor_copy(pair_col[:, :], pair_in[:, :, bass.ds(c, 1)].rearrange("p k a -> p (k a)")).then_inc(col_made, 1)
                    pool.tensor_copy(place_col[:, :], places_i[:, bass.ds(c, 1)]).then_inc(col_made, 1)
                    wait_alone(pool, col_made, 2 * c + 2)
                    pool.indirect_dma_start(pairs[:, :], bass.IndirectOffsetOnAxis(ap=place_col[:, :], axis=0),
                                            pair_col[:, :], None, bounds_check=E_PAD - 1, oob_is_err=False).then_inc(rewritten, 16)
                    wait_alone(pool, rewritten, 16 * c + 16)
                done = 16 * COLS
                pool.dma_start(pair_tile[:, :, :], pairs.rearrange("(p c) k -> p c k", p=P)).then_inc(rewritten, 16)
                pool.wait_ge(rewritten, done + 16)
                pool.tensor_copy(pair_in[:, 0, :], pair_tile[:, :, 0]).then_inc(apart, 1)
                pool.tensor_copy(pair_in[:, 1, :], pair_tile[:, :, 1]).then_inc(apart, 1)
                pool.wait_ge(apart, 2)
                pool.dma_start(whole(src_pad), pair_in[:, 0, :]).then_inc(rewritten, 16)
                pool.dma_start(whole(dst_pad[1:E_PAD + 1]), pair_in[:, 1, :]).then_inc(rewritten, 16)
                pool.wait_ge(rewritten, done + 48)
                pool.dma_start(all_dst[:, :], whole(dst_pad[1:E_PAD + 1])).then_inc(rewritten, 16)
                pool.wait_ge(rewritten, done + 64)

            pool.memset(zeros_i[:, :], 0).then_inc(pads_made, 1)
            pool.memset(ends_i[:, 0:P], -1).then_inc(pads_made, 1)
            pool.memset(ends_i[:, P:], N).then_inc(pads_made, 1)
            pool.memset(ident[:, :], 0.0).then_inc(ident_made, 1)
            pool.wait_ge(ident_made, 1)
            pool.affine_select(ident[:, :], ident[:, :], [[-1, P]], ALU.not_equal, 1.0, base=0,
                               channel_multiplier=1).then_inc(ident_made, 1)
            pool.iota(checked_to[:, :], [[NODES, GROUPS]], base=FIRST_CHECK, channel_multiplier=0).then_inc(checks_made, 1)
            pool.wait_ge(unsorted_made, 1)
            with pool.If(pool.value_load(unsorted[:, :]) > 0):
                place_edges()
                pool.sem_inc(in_order, 1)
            with pool.Else():
                pool.sem_inc(in_order, 1)
            for r in range(PEEL):
                gather(0, r)
            pool.wait_ge(any_far_made, 1)
            with pool.Fori(0, LOOPS) as i:
                for r in range(PEEL, PEEL + RING):
                    group(i, r)
            for g in range(GROUPS - PEEL, CHECKED):
                scatter_if_stored(0, g)
            pool.wait_ge(z_stored[(GROUPS - 1) % RING], stores_of((GROUPS - 1) % RING))
            for g in range(CHECKED, GROUPS):
                edge_rows_made(g)
                scatter(g % RING, edge_z[:, g % RING], out_i[:, g % RING], scattered[g % RING])
            for q in range(RING):
                pool.wait_ge(scattered[q], 16 * QUAD * sum(1 for g in range(GROUPS) if g % RING == q))
            pool.wait_ge(any_far_made, 1)
            with pool.If(pool.value_load(any_far[:, :]) > 0):
                with pool.Fori(0, CHECKED) as g:
                    with pool.If(near(g)):
                        idle = src_pad[0:EDGES].rearrange("(p j) -> p j", j=QUAD)
                        pool.dma_start(back_i[:, :], idle).then_inc(back_in, 32)
                        wait_alone(pool, back_in, 32 * g + 32)
                        pool.dma_start(back_i[:, :], idle).then_inc(back_out, 16 * QUAD)
                    with pool.Else():
                        rows = kept_rows[bass.ds(P * g, P), :].rearrange("p (j f) -> p j f", j=QUAD)
                        pool.dma_start(back_rows[:, :, :], rows).then_inc(back_in, 16)
                        pool.dma_start(back_i[:, :], kept_index[bass.ds(P * g, P), :]).then_inc(back_in, 16)
                        wait_alone(pool, back_in, 32 * g + 32)
                        scatter(0, back_rows, back_i, back_out)
                    wait_alone(pool, back_out, 16 * QUAD * g + 16 * QUAD)
            with pool.Else():
                pool.sem_inc(waits_passed, 1)


_INS = ["x", "src", "dst", "L0_gnn_msg_w1", "L0_gnn_msg_b1", "L0_gnn_msg_w2", "L0_gnn_msg_b2",
        "L0_gnn_upd_w1", "L0_gnn_upd_b1", "L0_gnn_upd_w2", "L0_gnn_upd_b2"]


def kernel(**inputs):
    import concourse.bacc as bacc
    from concourse.bass_utils import run_bass_kernel_spmd

    nc = bacc.Bacc("TRN2", target_bir_lowering=False, num_devices=1)
    arrays, args = {}, []
    for name in _INS:
        a = np.ascontiguousarray(inputs[name])
        arrays[f"in_{name}"] = a
        args.append(nc.dram_tensor(f"in_{name}", a.shape, mybir.dt.from_np(a.dtype), kind="ExternalInput").ap())
    shape = inputs["x"].shape
    args.append(nc.dram_tensor("out_0", shape, F32, kind="ExternalOutput").ap())
    gnn_resnorm(nc, *args)
    r = run_bass_kernel_spmd(nc, [arrays], core_ids=[0])
    return r.results[0]["out_0"]
```
